# Optimizing a Trainium2 kernel written in Bass

```python
import numpy as np
import jax
import jax.numpy as jnp

def _softmax(x, axis=-1):
    return jax.nn.softmax(x, axis=axis)

def _gelu(x):
    return jax.nn.gelu(x, approximate=True)

def _silu(x):
    return jax.nn.silu(x)

def _sigmoid(x):
    return jax.nn.sigmoid(x)

def _layernorm(x, axis=-1, eps=1e-05):
    m = jnp.mean(x, axis=axis, keepdims=True)
    v = jnp.var(x, axis=axis, keepdims=True)
    return (x - m) / jnp.sqrt(v + eps)

def _scatter_add(tgt, idx, src, axis=0):
    return tgt.at[idx].add(src)

def _segment_sum(src, seg, n):
    return jax.ops.segment_sum(src, seg, n)
kernel_name = 'mk_seq_preln_d1_jaxref_r8_e30e4d'

def setup_inputs(seed: int=0):
    np.random.seed(seed)
    _w = jnp.asarray

    def _L0_attn_setup():
        import jax, jax.numpy as jnp
        import numpy as np
        D_MODEL = 128
        N_HEADS = 16
        D_HEAD = 64
        VAR_EPS = 1e-05
        INIT_RANGE = 0.02
        B, S = (2, 256)

        def _layernorm(x, w, b):
            mean = jnp.mean(x, axis=-1, keepdims=True)
            var = jnp.var(x, axis=-1, keepdims=True)
            norm = (x - mean) / jnp.sqrt(var + VAR_EPS)
            return norm * w + b
        key = jax.random.key(seed)
        ks = jax.random.split(key, 6)
        resid_stream = jax.random.normal(ks[0], (B, S, D_MODEL), dtype=jnp.float32)
        attn_mask = jnp.ones((B, S), dtype=jnp.int32)
        W_q = jax.random.normal(ks[1], (N_HEADS, D_MODEL, D_HEAD), dtype=jnp.float32) * INIT_RANGE
        W_k = jax.random.normal(ks[2], (N_HEADS, D_MODEL, D_HEAD), dtype=jnp.float32) * INIT_RANGE
        W_v = jax.random.normal(ks[3], (N_HEADS, D_MODEL, D_HEAD), dtype=jnp.float32) * INIT_RANGE
        W_o = jax.random.normal(ks[4], (N_HEADS, D_HEAD, D_MODEL), dtype=jnp.float32) * INIT_RANGE
        b_q = jnp.zeros((N_HEADS, D_HEAD), dtype=jnp.float32)
        b_k = jnp.zeros((N_HEADS, D_HEAD), dtype=jnp.float32)
        b_v = jnp.zeros((N_HEADS, D_HEAD), dtype=jnp.float32)
        b_o = jnp.zeros((D_MODEL,), dtype=jnp.float32)
        ln_w = jnp.ones((D_MODEL,), dtype=jnp.float32)
        ln_b = jnp.zeros((D_MODEL,), dtype=jnp.float32)
        return dict(resid_stream=resid_stream, attn_mask=attn_mask, W_q=W_q, W_k=W_k, W_v=W_v, W_o=W_o, b_q=b_q, b_k=b_k, b_v=b_v, b_o=b_o, ln_w=ln_w, ln_b=ln_b)
    _L0_attn_in = _L0_attn_setup()

    def _L0_ffn_setup():
        import jax, jax.numpy as jnp
        import numpy as np
        B, S, D, H, M, E, K = (4, 256, 128, 256, 64, 8, 2)

        def _layernorm(x, g, b, eps=1e-05):
            mu = x.mean(-1, keepdims=True)
            var = ((x - mu) ** 2).mean(-1, keepdims=True)
            return (x - mu) * jax.lax.rsqrt(var + eps) * g + b

        def _forward(inputs_embeds, enc_W, enc_b, s2c_W, s2c_b, rW1, rb1, rW2, rb2, We1, be1, We2, be2, c2s_W, c2s_b, dec_W, dec_b, ln_g, ln_b):
            b, s, _ = inputs_embeds.shape
            spikes_enc = jax.nn.sigmoid(inputs_embeds @ enc_W + enc_b)
            flat = spikes_enc.reshape(b * s, H)
            cont = flat @ s2c_W + s2c_b
            logits = jnp.tanh(cont @ rW1 + rb1) @ rW2 + rb2
            probs = jax.nn.softmax(logits, axis=-1)
            topw, topi = jax.lax.top_k(probs, K)
            w = topw / topw.sum(-1, keepdims=True)
            gates = (jax.nn.one_hot(topi, E, dtype=cont.dtype) * w[..., None]).sum(1)
            h = jax.nn.relu(jnp.einsum('nm,emh->enh', cont, We1) + be1[:, None, :])
            expert_out = jnp.einsum('enh,ehm->enm', h, We2) + be2[:, None, :]
            output_flat = jnp.einsum('enm,ne->nm', expert_out, gates)
            spikes_moe = jax.nn.sigmoid(output_flat @ c2s_W + c2s_b).reshape(b, s, H)
            decoded = jax.nn.sigmoid(spikes_moe @ dec_W + dec_b)
            return _layernorm(decoded, ln_g, ln_b)
        key = jax.random.key(seed)
        ks = jax.random.split(key, 10)
        r = lambda k, shape: jax.random.normal(k, shape, dtype=jnp.float32) * 0.02
        return {'inputs_embeds': jax.random.normal(ks[0], (B, S, D), dtype=jnp.float32), 'enc_W': r(ks[1], (D, H)), 'enc_b': jnp.zeros((H,), jnp.float32), 's2c_W': r(ks[2], (H, M)), 's2c_b': jnp.zeros((M,), jnp.float32), 'rW1': r(ks[3], (M, 64)), 'rb1': jnp.zeros((64,), jnp.float32), 'rW2': r(ks[4], (64, E)), 'rb2': jnp.zeros((E,), jnp.float32), 'We1': r(ks[5], (E, M, H // 2)), 'be1': jnp.zeros((E, H // 2), jnp.float32), 'We2': r(ks[6], (E, H // 2, M)), 'be2': jnp.zeros((E, M), jnp.float32), 'c2s_W': r(ks[7], (M, H)), 'c2s_b': jnp.zeros((H,), jnp.float32), 'dec_W': r(ks[8], (H, D)), 'dec_b': jnp.zeros((D,), jnp.float32), 'ln_g': jnp.ones((D,), jnp.float32), 'ln_b': jnp.zeros((D,), jnp.float32)}
    _L0_ffn_in = _L0_ffn_setup()
    _d = {'L0_attn_resid_stream': _L0_attn_in['resid_stream'], 'L0_attn_attn_mask': _L0_attn_in['attn_mask'], 'L0_attn_W_q': _L0_attn_in['W_q'], 'L0_attn_W_k': _L0_attn_in['W_k'], 'L0_attn_W_v': _L0_attn_in['W_v'], 'L0_attn_W_o': _L0_attn_in['W_o'], 'L0_attn_b_q': _L0_attn_in['b_q'], 'L0_attn_b_k': _L0_attn_in['b_k'], 'L0_attn_b_v': _L0_attn_in['b_v'], 'L0_attn_b_o': _L0_attn_in['b_o'], 'L0_attn_ln_w': _L0_attn_in['ln_w'], 'L0_attn_ln_b': _L0_attn_in['ln_b'], 'L0_ffn_enc_W': _L0_ffn_in['enc_W'], 'L0_ffn_enc_b': _L0_ffn_in['enc_b'], 'L0_ffn_s2c_W': _L0_ffn_in['s2c_W'], 'L0_ffn_s2c_b': _L0_ffn_in['s2c_b'], 'L0_ffn_rW1': _L0_ffn_in['rW1'], 'L0_ffn_rb1': _L0_ffn_in['rb1'], 'L0_ffn_rW2': _L0_ffn_in['rW2'], 'L0_ffn_rb2': _L0_ffn_in['rb2'], 'L0_ffn_We1': _L0_ffn_in['We1'], 'L0_ffn_be1': _L0_ffn_in['be1'], 'L0_ffn_We2': _L0_ffn_in['We2'], 'L0_ffn_be2': _L0_ffn_in['be2'], 'L0_ffn_c2s_W': _L0_ffn_in['c2s_W'], 'L0_ffn_c2s_b': _L0_ffn_in['c2s_b'], 'L0_ffn_dec_W': _L0_ffn_in['dec_W'], 'L0_ffn_dec_b': _L0_ffn_in['dec_b'], 'L0_ffn_ln_g': _L0_ffn_in['ln_g'], 'L0_ffn_ln_b': _L0_ffn_in['ln_b']}
    _x0 = _d['L0_attn_resid_stream']
    _d['L0_attn_resid_stream'] = jax.random.normal(jax.random.fold_in(jax.random.key(seed), 1), (4, 1024, 128), dtype=_x0.dtype)
    del _x0
    return _d

def reference(L0_attn_resid_stream, L0_attn_attn_mask, L0_attn_W_q, L0_attn_W_k, L0_attn_W_v, L0_attn_W_o, L0_attn_b_q, L0_attn_b_k, L0_attn_b_v, L0_attn_b_o, L0_attn_ln_w, L0_attn_ln_b, L0_ffn_enc_W, L0_ffn_enc_b, L0_ffn_s2c_W, L0_ffn_s2c_b, L0_ffn_rW1, L0_ffn_rb1, L0_ffn_rW2, L0_ffn_rb2, L0_ffn_We1, L0_ffn_be1, L0_ffn_We2, L0_ffn_be2, L0_ffn_c2s_W, L0_ffn_c2s_b, L0_ffn_dec_W, L0_ffn_dec_b, L0_ffn_ln_g, L0_ffn_ln_b):

    def _L0_attn_ref(resid_stream, attn_mask, W_q, W_k, W_v, W_o, b_q, b_k, b_v, b_o, ln_w, ln_b):
        import jax, jax.numpy as jnp
        import numpy as np
        D_MODEL = 128
        N_HEADS = 16
        D_HEAD = 64
        VAR_EPS = 1e-05
        INIT_RANGE = 0.02
        B, S = (2, 256)

        def _layernorm(x, w, b):
            mean = jnp.mean(x, axis=-1, keepdims=True)
            var = jnp.var(x, axis=-1, keepdims=True)
            norm = (x - mean) / jnp.sqrt(var + VAR_EPS)
            return norm * w + b
        x = _layernorm(resid_stream, ln_w, ln_b)
        q = jnp.einsum('bsd,hde->bshe', x, W_q) + b_q
        k = jnp.einsum('bsd,hde->bshe', x, W_k) + b_k
        v = jnp.einsum('bsd,hde->bshe', x, W_v) + b_v
        scale = D_HEAD ** (-0.5)
        scores = jnp.einsum('bqhe,bkhe->bhqk', q, k) * scale
        sq, sk = (scores.shape[-2], scores.shape[-1])
        causal = jnp.tril(jnp.ones((sq, sk), dtype=bool))
        scores = jnp.where(causal, scores, -jnp.inf)
        pattern = jax.nn.softmax(scores, axis=-1)
        z = jnp.einsum('bhqk,bkhe->bqhe', pattern, v)
        attn_out = jnp.einsum('bqhe,hed->bqd', z, W_o) + b_o
        return attn_out

    def _L0_ffn_ref(inputs_embeds, enc_W, enc_b, s2c_W, s2c_b, rW1, rb1, rW2, rb2, We1, be1, We2, be2, c2s_W, c2s_b, dec_W, dec_b, ln_g, ln_b):
        import jax, jax.numpy as jnp
        import numpy as np
        B, S, D, H, M, E, K = (4, 256, 128, 256, 64, 8, 2)

        def _layernorm(x, g, b, eps=1e-05):
            mu = x.mean(-1, keepdims=True)
            var = ((x - mu) ** 2).mean(-1, keepdims=True)
            return (x - mu) * jax.lax.rsqrt(var + eps) * g + b

        def _forward(inputs_embeds, enc_W, enc_b, s2c_W, s2c_b, rW1, rb1, rW2, rb2, We1, be1, We2, be2, c2s_W, c2s_b, dec_W, dec_b, ln_g, ln_b):
            b, s, _ = inputs_embeds.shape
            spikes_enc = jax.nn.sigmoid(inputs_embeds @ enc_W + enc_b)
            flat = spikes_enc.reshape(b * s, H)
            cont = flat @ s2c_W + s2c_b
            logits = jnp.tanh(cont @ rW1 + rb1) @ rW2 + rb2
            probs = jax.nn.softmax(logits, axis=-1)
            topw, topi = jax.lax.top_k(probs, K)
            w = topw / topw.sum(-1, keepdims=True)
            gates = (jax.nn.one_hot(topi, E, dtype=cont.dtype) * w[..., None]).sum(1)
            h = jax.nn.relu(jnp.einsum('nm,emh->enh', cont, We1) + be1[:, None, :])
            expert_out = jnp.einsum('enh,ehm->enm', h, We2) + be2[:, None, :]
            output_flat = jnp.einsum('enm,ne->nm', expert_out, gates)
            spikes_moe = jax.nn.sigmoid(output_flat @ c2s_W + c2s_b).reshape(b, s, H)
            decoded = jax.nn.sigmoid(spikes_moe @ dec_W + dec_b)
            return _layernorm(decoded, ln_g, ln_b)
        return _forward(inputs_embeds, enc_W, enc_b, s2c_W, s2c_b, rW1, rb1, rW2, rb2, We1, be1, We2, be2, c2s_W, c2s_b, dec_W, dec_b, ln_g, ln_b)
    x = L0_attn_resid_stream
    x = x + _L0_attn_ref(_layernorm(x, axis=-1), L0_attn_attn_mask, L0_attn_W_q, L0_attn_W_k, L0_attn_W_v, L0_attn_W_o, L0_attn_b_q, L0_attn_b_k, L0_attn_b_v, L0_attn_b_o, L0_attn_ln_w, L0_attn_ln_b)
    x = x + _L0_ffn_ref(_layernorm(x, axis=-1), L0_ffn_enc_W, L0_ffn_enc_b, L0_ffn_s2c_W, L0_ffn_s2c_b, L0_ffn_rW1, L0_ffn_rb1, L0_ffn_rW2, L0_ffn_rb2, L0_ffn_We1, L0_ffn_be1, L0_ffn_We2, L0_ffn_be2, L0_ffn_c2s_W, L0_ffn_c2s_b, L0_ffn_dec_W, L0_ffn_dec_b, L0_ffn_ln_g, L0_ffn_ln_b)
    return x

_drawn_inputs = setup_inputs


def setup_inputs(seed=0):
    import zlib

    import numpy as np

    out = dict(_drawn_inputs(seed))
    spreads = {'L0_attn_b_q': (0.0, 0.8),
     'L0_attn_b_k': (0.0, 0.8),
     'L0_attn_b_v': (0.0, 0.1),
     'L0_attn_b_o': (0.0, 0.1),
     'L0_attn_ln_w': (1.0, 0.6),
     'L0_attn_ln_b': (0.0, 0.787),
     'L0_ffn_enc_b': (0.0, 0.8),
     'L0_ffn_s2c_b': (0.0, 0.8),
     'L0_ffn_rb1': (0.0, 0.8),
     'L0_ffn_rb2': (0.0, 0.8),
     'L0_ffn_be1': (0.0, 0.8),
     'L0_ffn_be2': (0.0, 0.8),
     'L0_ffn_c2s_b': (0.0, 0.276),
     'L0_ffn_dec_b': (0.0, 0.1),
     'L0_ffn_ln_g': (1.0, 0.2),
     'L0_ffn_ln_b': (0.0, 0.1)}
    factors = {'L0_attn_W_q': 8.0,
     'L0_attn_W_k': 8.0,
     'L0_attn_W_v': 4.164,
     'L0_ffn_enc_W': 8.0,
     'L0_ffn_s2c_W': 8.0,
     'L0_ffn_rW1': 8.0,
     'L0_ffn_rW2': 8.0,
     'L0_ffn_We1': 8.0,
     'L0_ffn_We2': 8.0,
     'L0_ffn_c2s_W': 8.0}
    for name, (base, spread) in spreads.items():
        noise = np.random.default_rng([zlib.crc32(name.encode()), seed]).standard_normal(out[name].shape)
        drawn = base * np.exp(spread * noise) if base else spread * noise
        out[name] = jnp.asarray(drawn.astype(out[name].dtype))
    for name, factor in factors.items():
        out[name] = (out[name] * factor).astype(out[name].dtype)
    return out
```

```python
from contextlib import ExitStack

import numpy as np
import concourse.bass as bass
from concourse import mybir

F32 = mybir.dt.float32
F32R = mybir.dt.float32r
ACT = mybir.ActivationFunctionType
ALU = mybir.AluOpType
AXIS_X = mybir.AxisListType.X

P = 128
B, S, D = 4, 1024, 128
NH, DH = 16, 64
HP = NH // 2
STEPS = B * HP
QT = S // P
UNITS = 2 * QT
NT = B * S // P
CH = 512
NC = B * S // CH
TC = CH // P
HID, M, E, EH = 256, 64, 8, 128
HB = HID // P
EPS = 1e-5
GSTEPS = 14
BIG = 3.0e38
TURNS = 8 + 16
HALF_TURNS = TURNS // 2


def build_program(nc, a, out):
    with ExitStack() as ctx:
        def sb(name, shape, dt=F32):
            return ctx.enter_context(nc.sbuf_tensor(name, shape, dt))

        def sem(name):
            return ctx.enter_context(nc.semaphore(name))

        X = sb("X", [P, NT, D])
        xt_dram = nc.dram_tensor("xt_scratch", (P, B * S), F32, kind="Internal").ap()
        IDENT = sb("IDENT", [P, P])
        MASK = sb("MASK", [P, S])
        WO = sb("WO", [P, HP, D])
        WV = sb("WV", [P, NH, DH])
        BV = sb("BV", [P, NH * DH])
        BO = sb("BO", [P, D])
        BQK = sb("BQK", [P, NH])
        QKSCALE = sb("QKSCALE", [P, 1])
        LNW = sb("LNW", [P, 1])
        LNB = sb("LNB", [P, 1])
        EPST = sb("EPST", [P, 1])
        WQK = [sb(f"WQK{i}", [P, 2, P]) for i in range(2)]
        XTB = [sb(f"XTB{i}", [P, S]) for i in range(2)]
        RAW = sb("RAW", [P, 2, CH])
        RH = sb("RH", [P, 2, S], F32R)
        RL = sb("RL", [P, 2, S], F32R)
        QS = [sb(f"QS{i}", [P, 2, S], F32R) for i in range(2)]
        KH = [sb(f"KH{i}", [P, 2, S], F32R) for i in range(2)]
        KL = [sb(f"KL{i}", [P, 2, S], F32R) for i in range(2)]
        V = [sb(f"V{i}", [P, QT, P]) for i in range(2)]
        SSB = [sb(f"SSB{i}", [P, S]) for i in range(2)]
        PR = [sb(f"PR{i}", [P, S]) for i in range(4)]
        NM = sb("NM", [P, 2 * UNITS])
        L = sb("L", [P, 2 * UNITS])
        RCP = sb("RCP", [P, 2, 8])
        RX = [sb(f"RX{i}", [P, TC, 2, DH]) for i in range(2)]
        RSB = [sb(f"RSB{i}", [P, CH]) for i in range(2)]
        ZN = [sb(f"ZN{i}", [P, CH]) for i in range(2)]
        PT = [sb("PT0", [P, 2, 4, CH]), sb("PT1", [P, 2, 8, CH])]
        ST = sb("ST", [P, TC, 6])
        MV = sb("MV", [P, TC, 2])
        SD = sb("SD", [P, TC])
        RS = sb("RS", [P, TC])
        Y = SSB[0][:, 0:CH].rearrange("p (t d) -> p t d", d=D)
        Y2 = SSB[1][:, 0:CH].rearrange("p (t d) -> p t d", d=D)
        XST = PR[0][:, 0:CH]

        LOWER = sb("LOWER", [P, E, E])

        WE1_RAW = XTB[0][:, :].rearrange("p (e h) -> p e h", e=E)
        W2 = XTB[1][:, 0:E * M].rearrange("p (e m) -> p e m", e=E)
        DECW = XTB[1][:, 512:768].rearrange("p (m d) -> p m d", m=HB)
        C2SW = XTB[1][:, 768:1024]
        wv = WV[:, :, :].rearrange("p h e -> p (h e)")
        ENCW = wv[:, 0:256]
        S2CW = wv[:, 256:512].rearrange("p (m c) -> p m c", m=HB)
        DECB = wv[:, 512:640]
        LNG = wv[:, 640:768]
        LNBB = wv[:, 768:896]
        RW1_RAW = wv[:, 896:1024]
        ENCB, S2CB, RB1 = BV[:, 0:2], BV[:, 2:3], BV[:, 3:4]
        RW2, RB2, BE1 = BV[:, 8:16], BV[:, 16:24], BV[:, 24:32]
        C2SB, BE2 = BV[:, 32:34], BV[:, 64:128]
        WE1 = QS[0][:, 0, :].rearrange("p (e h) -> p e h", e=E)
        RW1 = QS[0][:, 1, 0:P]
        HIGH = KL[0][:, 0, :]
        HIGH1 = KL[0][:, 1, 0:P]
        CH_, CL_ = KH[0][:, 0, 0:CH], KH[0][:, 1, 0:CH]
        F = [PT[1][:, i // 8, i % 8, :] for i in range(16)] + [PT[0][:, i // 4, i % 4, :] for i in range(8)]
        YT, ET, ES, C32, T1 = F[0], F[1:3], F[3:5], F[5], F[6]
        H, GH, O, SMT, SM = F[7:9], F[9:13], F[13], F[14:16], F[16:18]
        GT = F[18]
        tiled = lambda f: f.rearrange("p (t d) -> p t d", d=P)
        DD, DT, D2, GP = tiled(F[19]), tiled(F[20]), tiled(F[21]), tiled(F[22])
        YF = tiled(F[23])
        NRM, PRO, OUT = tiled(SSB[0][:, 0:CH]), tiled(SSB[0][:, CH:S]), tiled(SSB[1][:, 0:CH])
        small = lambda i, n=TC * E: SSB[1][:, CH + i:CH + i + n]
        per = lambda x: x.rearrange("p (t e) -> p t e", e=E)
        LG, LM, EX, PB, RK, G1 = (per(small(32 * i)) for i in range(6))
        MX, SUM, RSUM, GS, RG = (small(192 + 4 * i, TC) for i in range(5))
        GR = PR[0][:, 0:TC * E * E].rearrange("p (t e f) -> p t e f", e=E, f=E)
        EQ = PR[0][:, 256:256 + TC * E * E].rearrange("p (t e f) -> p t e f", e=E, f=E)
        ST2, MV2, SD2, RS2 = (sb("ST2", [P, TC, 6]), sb("MV2", [P, TC, 2]), sb("SD2", [P, TC]), sb("RS2", [P, TC]))

        SP_ = [ctx.enter_context(nc.psum_tensor(f"SPS{i}", [P, S], F32)) for i in range(2)]
        TB = [ctx.enter_context(nc.psum_tensor(f"TB{i}", [P, CH], F32)) for i in range(2)]
        Z = ctx.enter_context(nc.psum_tensor("Z", [P, CH], F32))
        MB = ctx.enter_context(nc.psum_tensor("MB", [P, CH], F32))

        GB = [SP_[0][:, 0:CH], SP_[0][:, CH:S]]
        A0, A1 = SP_[1][:, 0:CH], SP_[1][:, CH:S]

        const_loaded = sem("const_loaded")
        x_loaded = sem("x_loaded")
        scale_set = sem("scale_set")
        mask_step = sem("mask_step")
        pool_const = sem("pool_const")
        ln_stats = sem("ln_stats"); ln_aggr = sem("ln_aggr"); ln_sd = sem("ln_sd")
        ln_rs = sem("ln_rs"); ln_y = sem("ln_y")
        xt_turned = sem("xt_turned"); xt_ready = sem("xt_ready"); xt_stored = sem("xt_stored"); bo_added = sem("bo_added")
        staged = [sem(f"staged{i}") for i in range(2)]
        qks_ready = [sem(f"qks_ready{i}") for i in range(2)]
        qk_filled = sem("qk_filled"); qk_evac = sem("qk_evac")
        v_filled = sem("v_filled"); v_evac = sem("v_evac")
        rounded = sem("rounded"); split_done = sem("split_done")
        s_filled = sem("s_filled"); s_masked = sem("s_masked"); exp_done = sem("exp_done")
        t_filled = sem("t_filled"); t_copied_act = sem("t_copied_act"); t_copied_dve = sem("t_copied_dve")
        pv_done = sem("pv_done"); zn_done = sem("zn_done")
        rcp_done = sem("rcp_done"); rx_ready = sem("rx_ready")
        r_filled = sem("r_filled"); r_evac = sem("r_evac")
        out_filled = sem("out_filled"); out_evac = sem("out_evac")

        f_loaded = sem("f_loaded"); f_high = sem("f_high"); f_weights = sem("f_weights"); zeroed = sem("zeroed")
        f_stats = sem("f_stats"); f_aggr = sem("f_aggr"); f_sd = sem("f_sd"); f_rs = sem("f_rs"); f_y = sem("f_y")
        f_turned = sem("f_turned"); f_yt = sem("f_yt"); f_enc = sem("f_enc"); f_et = sem("f_et"); f_es = sem("f_es")
        f_s2c = sem("f_s2c"); f_c32 = sem("f_c32"); f_ch = sem("f_ch"); f_cl = sem("f_cl")
        f_r1 = sem("f_r1"); f_t1 = sem("f_t1"); f_lg = sem("f_lg"); gate_step = sem("gate_step"); f_ex = sem("f_ex")
        f_gates = sem("f_gates"); f_gt = sem("f_gt"); f_gtc = sem("f_gtc")
        f_h = sem("f_h"); f_g = sem("f_g"); f_relu = sem("f_relu"); f_gh = sem("f_gh"); f_w2 = sem("f_w2"); f_o = sem("f_o")
        f_c2s = sem("f_c2s"); f_smt = sem("f_smt"); f_sm = sem("f_sm"); f_dec = sem("f_dec")
        f_d = sem("f_d"); f_dt = sem("f_dt"); f_d2 = sem("f_d2")
        g_stats = sem("g_stats"); g_aggr = sem("g_aggr"); g_sd = sem("g_sd"); g_rs = sem("g_rs"); g_y = sem("g_y")
        f_scaled = sem("f_scaled"); f_shifted = sem("f_shifted"); f_out = sem("f_out"); stored = sem("stored")
        lower_set = sem("lower_set")

        def wait(eng, s, value):
            if not isinstance(value, int) or value > 0:
                eng.wait_ge(s, value)

        block = ctx.enter_context(nc.Block())

        def each_step(eng, body):
            body(0, 0, 0, True, False)
            with eng.Fori(0, STEPS // 2 - 1) as j:
                body(j * 2 + 1, j, 1, False, False)
                body(j * 2 + 2, j + 1, 0, False, False)
            body(STEPS - 1, STEPS // 2 - 1, 1, False, True)

        def turns_of(n):
            t = n // 2
            if n < 8:
                return [(n, 0, t + 1)]
            return [(8 + 2 * (n - 8), 0, 4), (9 + 2 * (n - 8), 4, t - 3)]

        def each_chunk(eng, body):
            body(0, False)
            with eng.Fori(1, NC - 1) as c:
                body(c, False)
            body(NC - 1, True)

        def each_norm(eng, body):
            body(0)
            with eng.Fori(1, NC) as c:
                body(c)

        FFN_LOADS = 26

        def stage(sp, it, par):
            pair = it % HP
            b = (it // HP) % B
            sp.dma_start(WQK[par][:, :, 0:DH], a["W_q"][bass.ds(pair * 2, 2), :, :].rearrange("h d e -> d h e")).then_inc(staged[par], 16)
            sp.dma_start(WQK[par][:, :, DH:P], a["W_k"][bass.ds(pair * 2, 2), :, :].rearrange("h d e -> d h e")).then_inc(staged[par], 16)
            sp.dma_start(XTB[par][:, :], xt_dram[:, bass.ds(b * S, S)]).then_inc(staged[par], 16)

        def spread(sp, it, half, par):
            sp.wait_ge(split_done, (it + 1) * 4)
            sp.nop(nofuse=True)
            wait(sp, s_filled, (it - 1) * UNITS)
            lo, hi = slice(0, DH), slice(DH, P)
            for dst, src in ((QS[par][lo], RH[lo]), (QS[par][hi], RL[lo]),
                             (KH[par][lo], RH[hi]), (KH[par][hi], RH[hi]),
                             (KL[par][lo], RL[hi]), (KL[par][hi], RL[hi])):
                sp.dma_start(dst.bitcast(F32), src.bitcast(F32)).then_inc(qks_ready[par], 16)

        @block.sync
        def _(sp):
            x_tiles = a["x"].rearrange("b (t p) d -> p (b t) d", p=P)
            for c in range(NC):
                sp.dma_start(X[:, c * TC:(c + 1) * TC, :], x_tiles[:, c * TC:(c + 1) * TC, :]).then_inc(x_loaded, 16)
                if c == 0:
                    sp.dma_start(LNW[:, :], a["ln_w"].rearrange("(d o) -> d o", o=1)).then_inc(const_loaded, 16)
                    sp.dma_start(LNB[:, :], a["ln_b"].rearrange("(d o) -> d o", o=1)).then_inc(const_loaded, 16)
            sp.dma_start(WO[:, :, :], a["W_o"].rearrange("(p h) e d -> (h e) p d", h=2)).then_inc(const_loaded, 16)
            sp.dma_start(WV[:, :, :], a["W_v"].rearrange("h d e -> d h e")).then_inc(const_loaded, 16)
            sp.dma_start(BV[:, :], a["b_v"].rearrange("h e -> (h e)").partition_broadcast(P)).then_inc(const_loaded, 16)
            sp.dma_start(BO[:, :], a["b_o"].partition_broadcast(P)).then_inc(const_loaded, 16)
            sp.dma_start(BQK[0:DH, :], a["b_q"].rearrange("h e -> e h"), allow_slow_non_contiguous=True).then_inc(const_loaded, 16)
            sp.dma_start(BQK[DH:P, :], a["b_k"].rearrange("h e -> e h"), allow_slow_non_contiguous=True).then_inc(const_loaded, 16)
            def store_xt(c):
                sp.wait_ge(xt_ready, c + 1)
                sp.dma_start(xt_dram[:, bass.ds(c * CH, CH)], XST).then_inc(xt_stored, 16)
            each_norm(sp, store_xt)
            sp.wait_ge(xt_stored, NC * 16)
            stage(sp, 0, 0)
            stage(sp, 1, 1)
            spread(sp, 0, 0, 0)

            def body(it, half, par, first, last):
                if not last:
                    sp.wait_ge(v_filled, (it + 1) * 2)
                    stage(sp, it + 2, par)
                    spread(sp, it + 1, None, 1 - par)
            each_step(sp, body)
            sp.wait_ge(v_filled, STEPS * 2)
            sp.wait_ge(v_evac, STEPS * 2)
            sp.wait_ge(staged[0], (STEPS // 2 + 1) * 48)
            sp.wait_ge(zeroed, 1)
            col = lambda x: x.rearrange("(o p) -> p o", o=1)
            n = 0
            for dst, src in [(WE1_RAW[r], a["We1"].rearrange("e m h -> m e h")) for r in (slice(0, M), slice(M, P))] + \
                    [(W2, a["We2"].rearrange("e h m -> h e m")), (DECW, a["dec_W"].rearrange("(m p) d -> p m d", p=P)),
                     (C2SW[0:M], a["c2s_W"]), (C2SW[M:P], a["c2s_W"]), (ENCW, a["enc_W"]),
                     (S2CW[:, :, 0:M], a["s2c_W"].rearrange("(m p) c -> p m c", p=P)),
                     (S2CW[:, :, M:P], a["s2c_W"].rearrange("(m p) c -> p m c", p=P)),
                     (DECB, a["dec_b"].partition_broadcast(P)), (LNG, a["ln_g"].partition_broadcast(P)),
                     (LNBB, a["ln_b2"].partition_broadcast(P)),
                     (RW1_RAW[0:M, 0:M], a["rW1"]), (RW1_RAW[M:P, 0:M], a["rW1"]),
                     (RW1_RAW[0:M, M:P], a["rW1"]), (RW1_RAW[M:P, M:P], a["rW1"]),
                     (S2CB[0:M], col(a["s2c_b"])), (S2CB[M:P], col(a["s2c_b"])),
                     (RB1[0:M], col(a["rb1"])), (RB1[M:P], col(a["rb1"])),
                     (RW2[0:M], a["rW2"]), (RB2, a["rb2"].partition_broadcast(P)),
                     (ENCB, a["enc_b"].rearrange("(m p) -> p m", p=P)), (C2SB, a["c2s_b"].rearrange("(m p) -> p m", p=P)),
                     (BE1, a["be1"].rearrange("e h -> h e")), (BE2[0:E], a["be2"])]:
                sp.dma_start(dst, src, allow_slow_non_contiguous=True).then_inc(f_loaded, 16)
                n += 1
            assert n == FFN_LOADS
            out_tiles = out.rearrange("b (t p) d -> p (b t) d", p=P)

            def store(c, last):
                sp.wait_ge(f_out, c + 1)
                sp.dma_start(out_tiles[:, bass.ds(c * TC, TC), :], OUT).then_inc(stored, 16)
            each_chunk(sp, store)
            sp.wait_ge(stored, NC * 16)

        def expand(gp, it, g):
            gp.wait_ge(rcp_done, it * 2 + g + 1)
            wait(gp, r_filled, it * 2 + (1 if g else -1))
            gp.nop(nofuse=True)
            gp.tensor_copy(RX[g][:, :, :, :], RCP[:, g, :].rearrange("p (t h) -> p t h", h=2).unsqueeze(3).broadcast_to([P, TC, 2, DH])).then_inc(rx_ready, 1)

        def split(gp, it, half_prev, par_prev, parts):
            if half_prev is not None and 0 in parts:
                gp.wait_ge(qks_ready[par_prev], (half_prev + 1) * 96)
            for s in parts:
                h, c = s // 2, s % 2
                part = slice(c * CH, (c + 1) * CH)
                gp.wait_ge(qk_evac, it * 4 + s + 1)
                gp.nop(nofuse=True)
                gp.tensor_copy(RH[:, h, part], RAW[:, s % 2, :]).then_inc(rounded, 1)
                gp.wait_ge(rounded, it * 4 + s + 1)
                gp.tensor_tensor(RL[:, h, part], RAW[:, s % 2, :], RH[:, h, part].bitcast(F32), ALU.subtract).then_inc(split_done, 1)

        @block.gpsimd
        def _(gp):
            gp.memset(IDENT[:, :], 0.0).then_inc(mask_step, 1)
            gp.memset(MASK[:, :], 0.0).then_inc(mask_step, 1)
            gp.wait_ge(mask_step, 2)
            gp.affine_select(out=IDENT[:, :], in_=IDENT[:, :], compare_op=ALU.not_equal, fill=1.0,
                             base=0, pattern=[[-1, P]], channel_multiplier=1).then_inc(pool_const, 1)
            gp.affine_select(out=MASK[:, S - P:S], in_=MASK[:, S - P:S], compare_op=ALU.is_ge, fill=BIG,
                             base=0, pattern=[[-1, P]], channel_multiplier=1).then_inc(pool_const, 1)
            gp.memset(LOWER[:, :, :], 1.0).then_inc(lower_set, 1)
            gp.wait_ge(lower_set, 1)
            gp.affine_select(out=LOWER[:, :, :], in_=LOWER[:, :, :], compare_op=ALU.is_gt, fill=0.0,
                             base=0, pattern=[[1, E], [-1, E]], channel_multiplier=0).then_inc(lower_set, 1)
            gp.wait_ge(const_loaded, 16 * 8)
            gp.wait_ge(scale_set, 3)
            gp.tensor_scalar(BQK[:, :], BQK[:, :], QKSCALE[:, 0:1], None, ALU.mult).then_inc(pool_const, 1)
            def add_bo(c):
                gp.wait_ge(ln_y, c * 2 + 1)
                gp.tensor_tensor(X[:, bass.ds(c * TC, TC), :], X[:, bass.ds(c * TC, TC), :],
                                 BO[:, :].unsqueeze(1).broadcast_to([P, TC, D]), ALU.add).then_inc(bo_added, 1)
            each_norm(gp, add_bo)
            split(gp, 0, None, None, range(4))

            def body(it, half, par, first, last):
                if not last:
                    split(gp, it + 1, half, par, (0, 1))
                if not first:
                    expand(gp, it - 1, 1)
                if not last:
                    split(gp, it + 1, half, par, (2, 3))
                expand(gp, it, 0)
            each_step(gp, body)
            expand(gp, STEPS - 1, 1)
            def finish(c, last):
                gp.wait_ge(g_y, c + 1)
                gp.tensor_tensor(PRO, NRM, LNG.unsqueeze(1).broadcast_to([P, TC, D]), ALU.mult).then_inc(f_scaled, 1)
                gp.wait_ge(f_scaled, c + 1)
                wait(gp, stored, c * 16)
                gp.tensor_tensor(OUT, PRO, LNBB.unsqueeze(1).broadcast_to([P, TC, D]), ALU.add).then_inc(f_shifted, 1)
                gp.wait_ge(f_shifted, c + 1)
                gp.tensor_tensor(OUT, OUT, X[:, bass.ds(c * TC, TC), :], ALU.add).then_inc(f_out, 1)
            each_chunk(gp, finish)

        def pe_qk(pe, it, half, par, s):
            h, c = s // 2, s % 2
            pe.matmul(MB[:, :], WQK[par][:, h, :], XTB[par][:, c * CH:(c + 1) * CH], start=True, stop=True).then_inc(qk_filled, 1)

        def pe_v(pe, it, par, s):
            for k in range(TC):
                t = s * TC + k
                last = pe.matmul(MB[:, k * P:(k + 1) * P], XTB[par][:, t * P:(t + 1) * P],
                                 WV[:, bass.ds((it % HP) * 2, 2), :].rearrange("p h e -> p (h e)"), start=True, stop=True)
            last.then_inc(v_filled, 1)

        def pe_scores(pe, it, par, n):
            t, h = n // 2, n % 2
            w = (t + 1) * P
            for c0 in range(0, w, CH):
                wc = max(min(CH, w - c0), 256)
                pe.matmul(SP_[n % 2][:, c0:c0 + wc], QS[par][:, h, t * P:(t + 1) * P], KH[par][:, h, c0:c0 + wc], start=True, stop=False)
                last = pe.matmul(SP_[n % 2][:, c0:c0 + wc], QS[par][:, h, t * P:(t + 1) * P], KL[par][:, h, c0:c0 + wc], start=False, stop=True)
            last.then_inc(s_filled, 1)

        def pe_turn(pe, it, n):
            pe.wait_ge(exp_done, it * UNITS + n + 1)
            for idx, j0, nb in turns_of(n):
                wait(pe, t_copied_act if idx % 2 == 0 else t_copied_dve, it * HALF_TURNS + idx // 2)
                for k in range(nb):
                    last = pe.transpose(TB[idx % 2][:, k * P:(k + 1) * P], PR[n % 4][:, (j0 + k) * P:(j0 + k + 1) * P], IDENT[:, :])
                last.then_inc(t_filled, 1)

        def pe_values(pe, it, par, g, j):
            if j == 0:
                done = it * HALF_TURNS + (4 if g == 0 else HALF_TURNS)
                pe.wait_ge(t_copied_act, done)
                pe.wait_ge(t_copied_dve, done)
                pe.wait_ge(v_evac, (it + 1) * 2)
                wait(pe, zn_done, it * 2 + g)
            off = (j - g * TC) * P if j >= g * TC else 0
            nj = (g + 1) * TC
            for h in range(2):
                last = pe.matmul(Z[h * DH:(h + 1) * DH, off:CH], V[par][:, j, h * DH:(h + 1) * DH], PT[g][:, h, j, off:CH],
                                 start=(j == 0), stop=(j == nj - 1))
            if j == nj - 1:
                last.then_inc(pv_done, 1)

        def pe_spread_sums(pe, it, g):
            pe.wait_ge(rx_ready, it * 2 + g + 1)
            for i in range(TC):
                last = pe.transpose(MB[:, i * P:(i + 1) * P], RX[g][:, i, :, :].rearrange("p h e -> p (h e)"), IDENT[:, :])
            last.then_inc(r_filled, 1)

        def pe_out(pe, it, g):
            pe.wait_ge(zn_done, it * 2 + g + 1)
            for i in range(TC):
                last = pe.matmul(MB[:, i * P:(i + 1) * P], ZN[g][:, i * P:(i + 1) * P],
                                 WO[:, bass.ds(it % HP, 1), :].rearrange("p o d -> p (o d)"), start=True, stop=True)
            last.then_inc(out_filled, 1)

        def pe_slot(pe, it, half, par, first, last, n):
            if n == 0:
                pe.wait_ge(qks_ready[par], (half + 1) * 96)
            wait(pe, s_masked, it * UNITS + n - 1)
            pe_scores(pe, it, par, n)
            if n < 4 and not last:
                if n == 0:
                    pe.wait_ge(v_evac, it * 2 + 2)
                    nhalf = half + 1 if par else half
                    pe.wait_ge(staged[1 - par], (nhalf + 1) * 48)
                else:
                    pe.wait_ge(qk_evac, it * 4 + 4 + n)
                pe_qk(pe, it + 1, None, 1 - par, n)
            if n == 5 and not first:
                if last:
                    pe.wait_ge(v_evac, it * 2 + 2)
                else:
                    pe.wait_ge(qk_evac, it * 4 + 8)
                pe_out(pe, it - 1, 0)
            if n == 7 and not first:
                pe.wait_ge(out_evac, it * 2 - 1)
                pe_spread_sums(pe, it - 1, 1)
            if n == 12:
                if first:
                    pe.wait_ge(qk_evac, 8)
                else:
                    pe.wait_ge(r_evac, it * 2)
                pe_spread_sums(pe, it, 0)
            if n == 13 and not first:
                pe.wait_ge(r_evac, it * 2 + 1)
                pe_out(pe, it - 1, 1)
            if n in (14, 15) and not last:
                if n == 14 and first:
                    pe.wait_ge(r_evac, 1)
                elif n == 14:
                    pe.wait_ge(out_evac, it * 2)
                else:
                    pe.wait_ge(v_evac, it * 2 + 3)
                pe_v(pe, it + 1, 1 - par, n - 14)
            if n >= 3:
                pe_turn(pe, it, n - 3)
            elif not first:
                pe_turn(pe, it - 1, UNITS + n - 3)
            if n in (4, 6, 8, 10) and not first:
                pe_values(pe, it - 1, 1 - par, 1, n - 4)
                pe_values(pe, it - 1, 1 - par, 1, n - 3)
            if n in (13, 15):
                pe_values(pe, it, par, 0, n - 13)
                pe_values(pe, it, par, 0, n - 12)

        def pe_norm_turn(pe, c):
            pe.wait_ge(f_y, c + 1)
            wait(pe, f_gtc, c)
            for k in range(TC):
                last = pe.transpose(A0[:, k * P:(k + 1) * P], YF[:, k, :], IDENT[:, :])
            last.then_inc(f_turned, 1)

        def pe_encode(pe, c):
            pe.wait_ge(f_yt, c + 1)
            wait(pe, gate_step, c * GSTEPS - GSTEPS + 1)
            for m, bank in ((0, A1), (1, A0)):
                pe.matmul(bank, ENCW[:, m * P:(m + 1) * P], YT, start=True, stop=True).then_inc(f_enc, 1)

        def pe_cont(pe, c):
            pe.wait_ge(f_es, c * 2 + 2)
            for m in range(HB):
                last = pe.matmul(A1, S2CW[:, m, :], ES[m], start=(m == 0), stop=(m == HB - 1))
            last.then_inc(f_s2c, 1)

        def pe_router(pe, c):
            pe.wait_ge(f_cl, c + 1)
            pe.matmul(A0, RW1, CH_, start=True, stop=False)
            pe.matmul(A0, RW1, CL_, start=False, stop=True).then_inc(f_r1, 1)

        def pe_logits(pe, c):
            pe.wait_ge(f_t1, c + 1)
            for k in range(TC):
                last = pe.matmul(A1[:, k * E:(k + 1) * E], T1[:, k * P:(k + 1) * P], RW2, start=True, stop=True)
            last.then_inc(f_lg, 1)

        def pe_gate_turn(pe, c):
            pe.wait_ge(f_gates, c + 1)
            for k in range(TC):
                last = pe.transpose(A0[:, k * P:(k + 1) * P], GP[:, k, :], IDENT[:, :])
            last.then_inc(f_gt, 1)

        def pe_hidden(pe, c, p):
            for e in (2 * p, 2 * p + 1):
                if e == 0:
                    wait(pe, f_smt, c * 2)
                elif e == 1:
                    wait(pe, f_d, c)
                else:
                    pe.wait_ge(f_relu, c * E + e - 1)
                pe.matmul(TB[e % 2][:, :], WE1[:, e, :], CH_, start=True, stop=False)
                pe.matmul(TB[e % 2][:, :], WE1[:, e, :], CL_, start=False, stop=True).then_inc(f_h, 1)
            for e in (2 * p, 2 * p + 1):
                wait(pe, f_gh, c * E + max(e - 1, 0))
                for k in range(TC):
                    last = pe.transpose(GB[e % 2][:, k * P:(k + 1) * P], GP[:, k, e:e + 1].broadcast_to([P, P]), IDENT[:, :])
                last.then_inc(f_g, 1)

        def pe_experts(pe, c, p):
            pe.wait_ge(f_gh, c * E + 2 * p + 2)
            if p == 0:
                wait(pe, f_o, c)
            for e in (2 * p, 2 * p + 1):
                last = pe.matmul(Z[(e % 2) * M:(e % 2 + 1) * M, :], W2[:, e, :], GH[e % 4], start=(p == 0), stop=(e == E - 1))
            if p == E // 2 - 1:
                pe.wait_ge(f_gtc, c + 1)
                last = pe.matmul(Z[0:M, :], BE2, GT, start=False, stop=True)
            last.then_inc(f_w2, 1)

        def pe_c2s(pe, c):
            pe.wait_ge(f_o, c + 1)
            pe.wait_ge(f_relu, c * E + 7)
            for m, bank in ((0, MB[:, :]), (1, TB[0][:, :])):
                pe.matmul(bank, C2SW[:, m * P:(m + 1) * P], O, start=True, stop=True).then_inc(f_c2s, 1)

        def pe_decode(pe, c):
            pe.wait_ge(f_sm, c * 2 + 2)
            pe.wait_ge(f_relu, c * E + 8)
            for k in range(TC):
                for m in range(HB):
                    last = pe.matmul(TB[1][:, k * P:(k + 1) * P], SM[m][:, k * P:(k + 1) * P], DECW[:, m, :], start=(m == 0), stop=(m == HB - 1))
            last.then_inc(f_dec, 1)

        @block.tensor
        def _(pe):
            pe.wait_ge(pool_const, 1)
            def turn_norm(c):
                pe.wait_ge(ln_y, c * 2 + 2)
                for k in range(TC):
                    last = pe.transpose(MB[:, k * P:(k + 1) * P], Y2[:, k, :], IDENT[:, :])
                last.then_inc(xt_turned, 1)
                pe.wait_ge(xt_ready, c + 1)
            each_norm(pe, turn_norm)
            pe.wait_ge(staged[0], 48)
            pe.wait_ge(const_loaded, 16 * 8)
            for s in range(4):
                wait(pe, qk_evac, s)
                pe_qk(pe, 0, 0, 0, s)
            for s in range(2):
                wait(pe, qk_evac, 4) if s == 0 else pe.wait_ge(v_evac, 1)
                pe_v(pe, 0, 0, s)

            def body(it, half, par, first, last):
                for n in range(UNITS):
                    pe_slot(pe, it, half, par, first, last, n)
            each_step(pe, body)
            it, par = STEPS - 1, 1
            for n in range(3):
                pe_turn(pe, it, UNITS + n - 3)
            pe.wait_ge(r_evac, STEPS * 2 - 1)
            pe_out(pe, it, 0)
            for j in range(QT):
                pe_values(pe, it, par, 1, j)
            pe.wait_ge(out_evac, STEPS * 2 - 1)
            pe_spread_sums(pe, STEPS - 1, 1)
            pe.wait_ge(r_evac, STEPS * 2)
            pe_out(pe, it, 1)

            pe.wait_ge(f_weights, 6)
            pe_norm_turn(pe, 0)
            pe_encode(pe, 0)
            pe_cont(pe, 0)
            pe_router(pe, 0)
            pe_logits(pe, 0)
            pe_gate_turn(pe, 0)

            def chunk(c, last):
                pe_hidden(pe, c, 0)
                if not last:
                    pe_norm_turn(pe, c + 1)
                pe_hidden(pe, c, 1)
                pe_experts(pe, c, 0)
                if not last:
                    pe_encode(pe, c + 1)
                pe_hidden(pe, c, 2)
                pe_experts(pe, c, 1)
                pe_hidden(pe, c, 3)
                pe_experts(pe, c, 2)
                if not last:
                    pe_cont(pe, c + 1)
                pe_experts(pe, c, 3)
                pe_c2s(pe, c)
                if not last:
                    pe_router(pe, c + 1)
                pe_decode(pe, c)
                if not last:
                    pe_logits(pe, c + 1)
                    pe_gate_turn(pe, c + 1)
            each_chunk(pe, chunk)

        def copy_turn(eng, which, it, n):
            t, h = n // 2, n % 2
            g, tq = t // TC, t % TC
            for idx, j0, nb in turns_of(n):
                if idx % 2 == which:
                    eng.wait_ge(t_filled, it * TURNS + idx + 1)
                    dst = PT[g][:, h, j0:j0 + nb, tq * P:(tq + 1) * P]
                    src = TB[idx % 2][:, 0:nb * P].rearrange("p (j q) -> p j q", q=P)
                    if which == 0:
                        eng.activation(dst, src, ACT.Copy).then_inc(t_copied_act, 1)
                    else:
                        eng.tensor_copy(dst, src).then_inc(t_copied_dve, 1)

        def dve_reciprocal(v, it, g, par):
            v.wait_ge(exp_done, it * UNITS + 8 * g + 8)
            wait(v, rx_ready, it * 2 + (1 if g else -1))
            c0 = par * UNITS + g * 8
            v.reciprocal(RCP[:, g, :], L[:, c0:c0 + 8]).then_inc(rcp_done, 1)

        def dve_zn(v, it, g):
            v.wait_ge(pv_done, it * 2 + g + 1)
            v.wait_ge(r_evac, it * 2 + g + 1)
            v.tensor_tensor(ZN[g][:, :], Z[:, :], RSB[g][:, :], ALU.mult).then_inc(zn_done, 1)

        def dve_out(v, it, g):
            v.wait_ge(out_filled, it * 2 + g + 1)
            xs = X[:, bass.ds((it // HP) * QT + g * TC, TC), :]
            v.tensor_tensor(xs, xs, MB[:, :].rearrange("p (t d) -> p t d", d=D), ALU.add).then_inc(out_evac, 1)

        def dve_v(v, it, par, s):
            v.wait_ge(v_filled, it * 2 + s + 1)
            wait(v, pv_done, (it - 1) * 2)
            v.tensor_tensor(V[par][:, s * TC:(s + 1) * TC, :], MB[:, :].rearrange("p (t d) -> p t d", d=P),
                            BV[:, bass.ds((it % HP) * P, P)].unsqueeze(1).broadcast_to([P, TC, P]), ALU.add).then_inc(v_evac, 1)

        def dve_prepare(v):
            v.wait_ge(f_loaded, FFN_LOADS * 16)
            for raw, high, stack in ((XTB[0][:, :], HIGH, QS[0][:, 0, :]), (RW1_RAW, HIGH1, RW1)):
                v.tensor_copy(high, raw).then_inc(f_high, 1)
                v.tensor_copy(stack[0:M], raw[0:M]).then_inc(f_weights, 1)
            v.wait_ge(f_high, 2)
            for raw, high, stack in ((XTB[0][:, :], HIGH, QS[0][:, 0, :]), (RW1_RAW, HIGH1, RW1)):
                v.tensor_tensor(stack[M:P], raw[M:P], high[M:P].bitcast(F32), ALU.subtract).then_inc(f_weights, 1)
            v.tensor_scalar(ENCB, ENCB, 0.5, None, ALU.mult).then_inc(f_weights, 1)
            v.tensor_scalar(C2SB, C2SB, 0.5, None, ALU.mult).then_inc(f_weights, 1)

        def dve_slot(v, it, half, par, first, last, n):
            w = (n // 2 + 1) * P
            v.wait_ge(s_filled, it * UNITS + n + 1)
            wait(v, exp_done, it * UNITS + n - 1)
            v.nop(nofuse=True)
            v.tensor_tensor_reduce(out=SSB[n % 2][:, 0:w], in0=SP_[n % 2][:, 0:w], in1=MASK[:, S - w:S], scale=1.0, scalar=BIG,
                                   op0=ALU.add, op1=ALU.min, accum_out=NM[:, par * UNITS + n:par * UNITS + n + 1]).then_inc(s_masked, 1)
            if not first:
                if n == 0:
                    dve_zn(v, it - 1, 0)
                if n == 1:
                    dve_reciprocal(v, it - 1, 1, 1 - par)
                if n == 5:
                    dve_out(v, it - 1, 0)
                if n == 11:
                    dve_zn(v, it - 1, 1)
                if n == 13:
                    dve_out(v, it - 1, 1)
            if n == 9:
                dve_reciprocal(v, it, 0, par)
            if n in (14, 15) and not last:
                dve_v(v, it + 1, 1 - par, n - 14)
            if last and n == 0:
                v.wait_ge(v_evac, STEPS * 2)
                v.memset(BV[:, 0:P], 0.0).then_inc(zeroed, 1)
            if last and n == 14:
                dve_prepare(v)
            if n >= 3:
                copy_turn(v, 1, it, n - 3)
            elif not first:
                copy_turn(v, 1, it - 1, UNITS + n - 3)

        def norm_stats(v, src_tile, k0):
            for k in range(TC):
                v.bn_stats(ST[:, k, :], src_tile(k)).then_inc(ln_stats, 1)
            for k in range(TC):
                v.wait_ge(ln_stats, k0 * TC + k + 1)
                v.nop(nofuse=True)
                v.bn_aggr(MV[:, k, :], ST[:, k, :]).then_inc(ln_aggr, 1)

        def norm_apply(v, dst, src_tile, k0):
            v.wait_ge(ln_sd, k0 + 1)
            v.reciprocal(RS[:, :], SD[:, :]).then_inc(ln_rs, 1)
            v.wait_ge(ln_rs, k0 + 1)
            for k in range(TC):
                last = v.tensor_scalar(dst(k), src_tile(k), MV[:, k, 0:1], RS[:, k:k + 1], ALU.subtract, ALU.mult)
            last.then_inc(ln_y, 1)

        def stats(v, src, c, st, mv, s_stats, s_aggr):
            for k in range(TC):
                v.bn_stats(st[:, k, :], src(k)).then_inc(s_stats, 1)
            for k in range(TC):
                v.wait_ge(s_stats, c * TC + k + 1)
                v.nop(nofuse=True)
                v.bn_aggr(mv[:, k, :], st[:, k, :]).then_inc(s_aggr, 1)

        def apply(v, dst, src, c, mv, sd, rs, s_sd, s_rs, s_y):
            v.wait_ge(s_sd, c + 1)
            v.reciprocal(rs[:, :], sd[:, :]).then_inc(s_rs, 1)
            v.wait_ge(s_rs, c + 1)
            for k in range(TC):
                last = v.tensor_scalar(dst(k), src(k), mv[:, k, 0:1], rs[:, k:k + 1], ALU.subtract, ALU.mult)
            last.then_inc(s_y, 1)

        def x_tile(c):
            return lambda k: X[:, bass.ds(c * TC + k, 1), :].rearrange("p o d -> p (o d)")

        def norm_in(v, c):
            stats(v, x_tile(c), c, ST, MV, f_stats, f_aggr)

        def norm_in_apply(v, c):
            wait(v, f_turned, c)
            apply(v, lambda k: YF[:, k, :], x_tile(c), c, MV, SD, RS, f_sd, f_rs, f_y)

        def dve_affine(v, dst, src, ready, done, c):
            for m in range(HB):
                v.wait_ge(ready, c * 2 + m + 1)
                v.tensor_scalar(dst[m], src[m], 0.5, 0.5, ALU.mult, ALU.add).then_inc(done, 1)

        def dve_cont(v, c):
            v.wait_ge(f_c32, c + 1)
            wait(v, f_h, c * E)
            v.tensor_copy(CH_, C32).then_inc(f_ch, 1)
            v.wait_ge(f_ch, c + 1)
            v.tensor_tensor(CL_, C32, CH_.bitcast(F32), ALU.subtract).then_inc(f_cl, 1)

        def gates_1(v, c):
            v.wait_ge(f_lg, c + 1)
            s = c * GSTEPS
            v.tensor_tensor(LG, per(A1[:, 0:TC * E]), RB2.unsqueeze(1).broadcast_to([P, TC, E]), ALU.add).then_inc(gate_step, 1)
            v.wait_ge(gate_step, s + 1)
            v.tensor_reduce(MX, LG, AXIS_X, ALU.max).then_inc(gate_step, 1)
            v.wait_ge(gate_step, s + 2)
            v.tensor_tensor(LM, LG, MX.unsqueeze(2).broadcast_to([P, TC, E]), ALU.subtract).then_inc(gate_step, 1)

        def gates_2(v, c):
            s = c * GSTEPS + 3
            over = lambda x: x.unsqueeze(2).broadcast_to([P, TC, E])
            first = PB.unsqueeze(3).broadcast_to([P, TC, E, E])
            other = PB.unsqueeze(2).broadcast_to([P, TC, E, E])

            def step(op, n):
                op.then_inc(gate_step, 1)
                v.wait_ge(gate_step, s + n)
            v.wait_ge(f_ex, c + 1)
            step(v.tensor_reduce(SUM, EX, AXIS_X, ALU.add), 1)
            step(v.reciprocal(RSUM, SUM), 2)
            step(v.tensor_tensor(PB, EX, over(RSUM), ALU.mult), 3)
            step(v.tensor_tensor(EQ, other, first, ALU.is_equal), 4)
            step(v.tensor_tensor(EQ, EQ, LOWER[:, :, :].unsqueeze(1).broadcast_to([P, TC, E, E]), ALU.mult), 5)
            step(v.tensor_tensor(GR, other, first, ALU.is_gt), 6)
            step(v.tensor_tensor(GR, GR, EQ, ALU.add), 7)
            step(v.tensor_reduce(RK, GR, AXIS_X, ALU.add), 8)
            step(v.scalar_tensor_tensor(G1, RK, 1.5, PB, ALU.is_lt, ALU.mult), 9)
            step(v.tensor_reduce(GS, G1, AXIS_X, ALU.add), 10)
            step(v.reciprocal(RG, GS), 11)
            wait(v, f_g, c * E)
            v.tensor_tensor(GP[:, :, 0:E], G1, over(RG), ALU.mult).then_inc(f_gates, 1)

        def dve_gate(v, c, e):
            v.wait_ge(f_relu, c * E + e + 1)
            v.wait_ge(f_g, c * E + e + 1)
            wait(v, f_w2, c * 4 + max((e - 4) // 2 + 1, 0))
            v.tensor_tensor(GH[e % 4], H[e % 2], GB[e % 2], ALU.mult).then_inc(f_gh, 1)

        @block.vector
        def _(v):
            v.memset(QKSCALE[0:DH, :], -(DH ** -0.5)).then_inc(scale_set, 1)
            v.memset(QKSCALE[DH:P, :], 1.0).then_inc(scale_set, 1)
            v.memset(EPST[:, :], EPS).then_inc(scale_set, 1)
            v.wait_ge(x_loaded, NC * 16)

            def norm_twice(c):
                tile = lambda k: X[:, bass.ds(c * TC + k, 1), :].rearrange("p o d -> p (o d)")
                norm_stats(v, tile, c * 2)
                norm_apply(v, lambda k: Y[:, k, :], tile, c * 2)
                v.wait_ge(ln_y, c * 2 + 1)
                norm_stats(v, lambda k: Y[:, k, :], c * 2 + 1)
                wait(v, xt_turned, c)
                norm_apply(v, lambda k: Y2[:, k, :], lambda k: Y[:, k, :], c * 2 + 1)
            each_norm(v, norm_twice)
            v.wait_ge(const_loaded, 16 * 8)
            v.wait_ge(pool_const, 2)
            v.wait_ge(bo_added, NC)
            for s in range(2):
                dve_v(v, 0, 0, s)

            def body(it, half, par, first, last):
                for n in range(UNITS):
                    dve_slot(v, it, half, par, first, last, n)
            each_step(v, body)
            it = STEPS - 1
            dve_zn(v, it, 0)
            for n in range(3):
                copy_turn(v, 1, it, UNITS + n - 3)
            dve_out(v, it, 0)
            dve_reciprocal(v, it, 1, 1)
            dve_zn(v, it, 1)
            dve_out(v, it, 1)

            v.wait_ge(out_evac, STEPS * 2)
            v.memset(F[22], 0.0).then_inc(zeroed, 1)
            norm_in(v, 0)
            norm_in_apply(v, 0)
            dve_affine(v, ES, ET, f_et, f_es, 0)
            dve_cont(v, 0)
            gates_1(v, 0)
            gates_2(v, 0)

            def chunk(c, last):
                if not last:
                    norm_in(v, c + 1)
                dve_gate(v, c, 0)
                dve_gate(v, c, 1)
                if not last:
                    norm_in_apply(v, c + 1)
                for e in range(2, 6):
                    dve_gate(v, c, e)
                if not last:
                    dve_affine(v, ES, ET, f_et, f_es, c + 1)
                dve_gate(v, c, 6)
                dve_gate(v, c, 7)
                if not last:
                    dve_cont(v, c + 1)
                dve_affine(v, SM, SMT, f_smt, f_sm, c)
                v.wait_ge(f_dec, c + 1)
                v.tensor_tensor(DD, tiled(TB[1][:, :]), DECB.unsqueeze(1).broadcast_to([P, TC, D]), ALU.add).then_inc(f_d, 1)
                if not last:
                    gates_1(v, c + 1)
                v.wait_ge(f_dt, c + 1)
                v.tensor_scalar(D2, DT, 0.5, 0.5, ALU.mult, ALU.add).then_inc(f_d2, 1)
                v.wait_ge(f_d2, c + 1)
                stats(v, lambda k: D2[:, k, :], c, ST2, MV2, g_stats, g_aggr)
                if not last:
                    gates_2(v, c + 1)
                wait(v, f_scaled, c)
                apply(v, lambda k: NRM[:, k, :], lambda k: D2[:, k, :], c, MV2, SD2, RS2, g_sd, g_rs, g_y)
            each_chunk(v, chunk)

        def act_qk(act, it, s):
            h, c = s // 2, s % 2
            act.wait_ge(qk_filled, it * 4 + s + 1)
            wait(act, split_done, it * 4 + s - 1)
            act.nop(nofuse=True)
            act.activation(RAW[:, s % 2, :], MB[:, :], ACT.Identity,
                           bias=BQK[:, bass.ds((it % HP) * 2 + h, 1)], scale=QKSCALE[:, 0:1]).then_inc(qk_evac, 1)

        def act_sums(act, it, g):
            act.wait_ge(r_filled, it * 2 + g + 1)
            wait(act, zn_done, it * 2 + (1 if g else -1))
            act.activation(RSB[g][:, :], MB[:, :], ACT.Copy).then_inc(r_evac, 1)

        def act_slot(act, it, half, par, first, last, n):
            if n < 4 and not last:
                act_qk(act, it + 1, n)
            if n == 7 and not first:
                act_sums(act, it - 1, 1)
            if n == 12:
                act_sums(act, it, 0)
            if n >= 3:
                copy_turn(act, 0, it, n - 3)
            elif not first:
                copy_turn(act, 0, it - 1, UNITS + n - 3)
            w = (n // 2 + 1) * P
            col = par * UNITS + n
            act.wait_ge(s_masked, it * UNITS + n + 1)
            if n >= 4:
                act.wait_ge(t_filled, it * TURNS + turns_of(n - 4)[-1][0] + 1)
            elif not first:
                act.wait_ge(t_filled, (it - 1) * TURNS + turns_of(UNITS + n - 4)[-1][0] + 1)
            act.activation(PR[n % 4][:, 0:w], SSB[n % 2][:, 0:w], ACT.Exp, bias=NM[:, col:col + 1], scale=-1.0,
                           accum_out=L[:, col:col + 1]).then_inc(exp_done, 1)

        @block.scalar
        def _(act):
            act.wait_ge(scale_set, 3)
            act.wait_ge(const_loaded, 16 * 8)

            def norm_in_act(c):
                for r in range(2):
                    act.wait_ge(ln_aggr, c * 2 * TC + (r + 1) * TC)
                    act.activation(SD[:, :], MV[:, :, 1], ACT.Sqrt, bias=EPST[:, 0:1]).then_inc(ln_sd, 1)
                act.wait_ge(xt_turned, c + 1)
                wait(act, xt_stored, c * 16)
                act.activation(XST, MB[:, :], ACT.Identity, bias=LNB[:, 0:1], scale=LNW[:, 0:1]).then_inc(xt_ready, 1)
            each_norm(act, norm_in_act)
            act.wait_ge(pool_const, 3)
            for s in range(4):
                act_qk(act, 0, s)

            def body(it, half, par, first, last):
                for n in range(UNITS):
                    act_slot(act, it, half, par, first, last, n)
            each_step(act, body)
            it = STEPS - 1
            for n in range(3):
                copy_turn(act, 0, it, UNITS + n - 3)
            act_sums(act, it, 1)

            act.wait_ge(f_weights, 6)

            def deviation(c, mv, sd, aggr, done):
                act.wait_ge(aggr, (c + 1) * TC)
                act.activation(sd[:, :], mv[:, :, 1], ACT.Sqrt, bias=EPST[:, 0:1]).then_inc(done, 1)

            def first_a(c):
                act.wait_ge(f_turned, c + 1)
                act.activation(YT, A0, ACT.Copy).then_inc(f_yt, 1)

            def first_b(c):
                for m, bank in ((0, A1), (1, A0)):
                    act.wait_ge(f_enc, c * 2 + m + 1)
                    act.activation(ET[m], bank, ACT.Tanh, bias=ENCB[:, m:m + 1], scale=0.5).then_inc(f_et, 1)

            def first_c(c):
                act.wait_ge(f_s2c, c + 1)
                act.activation(C32, A1, ACT.Identity, bias=S2CB).then_inc(f_c32, 1)

            def first_d(c):
                act.wait_ge(f_r1, c + 1)
                act.activation(T1, A0, ACT.Tanh, bias=RB1).then_inc(f_t1, 1)

            def first_e(c):
                act.wait_ge(gate_step, c * GSTEPS + 3)
                act.activation(EX, LM, ACT.Exp).then_inc(f_ex, 1)

            def first_f(c):
                act.wait_ge(f_gt, c + 1)
                act.activation(GT, A0, ACT.Copy).then_inc(f_gtc, 1)

            def hidden(c, e):
                act.wait_ge(f_h, c * E + e + 1)
                wait(act, f_gh, c * E + max(e - 1, 0))
                act.activation(H[e % 2], TB[e % 2][:, :], ACT.Relu, bias=BE1[:, e:e + 1]).then_inc(f_relu, 1)

            deviation(0, MV, SD, f_aggr, f_sd)
            first_a(0)
            first_b(0)
            first_c(0)
            first_d(0)
            first_e(0)
            first_f(0)

            def chunk(c, last):
                if not last:
                    deviation(c + 1, MV, SD, f_aggr, f_sd)
                hidden(c, 0)
                hidden(c, 1)
                if not last:
                    first_a(c + 1)
                hidden(c, 2)
                hidden(c, 3)
                if not last:
                    first_b(c + 1)
                for e in range(4, 8):
                    hidden(c, e)
                if not last:
                    first_c(c + 1)
                act.wait_ge(f_w2, c * 4 + 4)
                act.activation(O, Z[:, :], ACT.Copy).then_inc(f_o, 1)
                for m, bank in ((0, MB[:, :]), (1, TB[0][:, :])):
                    act.wait_ge(f_c2s, c * 2 + m + 1)
                    act.activation(SMT[m], bank, ACT.Tanh, bias=C2SB[:, m:m + 1], scale=0.5).then_inc(f_smt, 1)
                if not last:
                    first_d(c + 1)
                act.wait_ge(f_d, c + 1)
                act.activation(DT, DD, ACT.Tanh, scale=0.5).then_inc(f_dt, 1)
                if not last:
                    first_e(c + 1)
                deviation(c, MV2, SD2, g_aggr, g_sd)
                if not last:
                    first_f(c + 1)
            each_chunk(act, chunk)


_NAMES = {
    "x": "L0_attn_resid_stream", "W_q": "L0_attn_W_q", "W_k": "L0_attn_W_k", "W_v": "L0_attn_W_v", "W_o": "L0_attn_W_o",
    "b_q": "L0_attn_b_q", "b_k": "L0_attn_b_k", "b_v": "L0_attn_b_v", "b_o": "L0_attn_b_o", "ln_w": "L0_attn_ln_w",
    "ln_b": "L0_attn_ln_b", "enc_W": "L0_ffn_enc_W", "enc_b": "L0_ffn_enc_b", "s2c_W": "L0_ffn_s2c_W", "s2c_b": "L0_ffn_s2c_b",
    "rW1": "L0_ffn_rW1", "rb1": "L0_ffn_rb1", "rW2": "L0_ffn_rW2", "rb2": "L0_ffn_rb2", "We1": "L0_ffn_We1", "be1": "L0_ffn_be1",
    "We2": "L0_ffn_We2", "be2": "L0_ffn_be2", "c2s_W": "L0_ffn_c2s_W", "c2s_b": "L0_ffn_c2s_b", "dec_W": "L0_ffn_dec_W",
    "dec_b": "L0_ffn_dec_b", "ln_g": "L0_ffn_ln_g", "ln_b2": "L0_ffn_ln_b",
}


def kernel(**inputs):
    import concourse.bacc as bacc
    from concourse.bass_utils import run_bass_kernel_spmd

    nc = bacc.Bacc("TRN2", target_bir_lowering=False, num_devices=1)
    arrays, args = {}, {}
    for short, name in _NAMES.items():
        arr = np.ascontiguousarray(inputs[name])
        arrays[f"in_{short}"] = arr
        args[short] = nc.dram_tensor(f"in_{short}", arr.shape, mybir.dt.from_np(arr.dtype), kind="ExternalInput").ap()
    out = nc.dram_tensor("out_x", (B, S, D), F32, kind="ExternalOutput").ap()
    build_program(nc, args, out)
    r = run_bass_kernel_spmd(nc, [arrays], core_ids=[0])
    return r.results[0]["out_x"]
```

```python
from contextlib import ExitStack

import numpy as np
import concourse.bass as bass
from concourse import mybir

F32 = mybir.dt.float32
F32R = mybir.dt.float32r
ACT = mybir.ActivationFunctionType
ALU = mybir.AluOpType
AXIS_X = mybir.AxisListType.X

P = 128
B, S, D = 4, 1024, 128
NH, DH = 16, 64
HP = NH // 2
STEPS = B * HP
QT = S // P
UNITS = 2 * QT
NT = B * S // P
CH = 512
NC = B * S // CH
TC = CH // P
HID, M, E, EH = 256, 64, 8, 128
HB = HID // P
EPS = 1e-5
GSTEPS = 14
BIG = 3.0e38
TURNS = 8 + 16
HALF_TURNS = TURNS // 2


def build_program(nc, a, out):
    with ExitStack() as ctx:
        def sb(name, shape, dt=F32):
            return ctx.enter_context(nc.sbuf_tensor(name, shape, dt))

        def sem(name):
            return ctx.enter_context(nc.semaphore(name))

        X = sb("X", [P, NT, D])
        xt_dram = nc.dram_tensor("xt_scratch", (P, B * S), F32, kind="Internal").ap()
        IDENT = sb("IDENT", [P, P])
        MASK = sb("MASK", [P, S])
        WO = sb("WO", [P, HP, D])
        WV = sb("WV", [P, NH, DH])
        BV = sb("BV", [P, NH * DH])
        BO = sb("BO", [P, D])
        BQK = sb("BQK", [P, NH])
        BQKS = [sb(f"BQKS{i}", [P, 2]) for i in range(2)]
        QKSCALE = sb("QKSCALE", [P, 1])
        LNW = sb("LNW", [P, 1])
        LNB = sb("LNB", [P, 1])
        EPST = sb("EPST", [P, 1])
        EPS4 = sb("EPS4", [P, 1])
        WQK = [sb(f"WQK{i}", [P, 2, P]) for i in range(2)]
        XTB = [sb(f"XTB{i}", [P, S]) for i in range(2)]
        RAW = sb("RAW", [P, 2, CH])
        RH = sb("RH", [P, 2, S], F32R)
        RL = sb("RL", [P, 2, S], F32R)
        QS = [sb(f"QS{i}", [P, 2, S], F32R) for i in range(2)]
        KH = [sb(f"KH{i}", [P, 2, S], F32R) for i in range(2)]
        KL = [sb(f"KL{i}", [P, 2, S], F32R) for i in range(2)]
        V = [sb(f"V{i}", [P, QT, P]) for i in range(2)]
        SSB = [sb(f"SSB{i}", [P, S]) for i in range(2)]
        PR = [sb(f"PR{i}", [P, S]) for i in range(4)]
        NM = sb("NM", [P, 2 * UNITS])
        L = sb("L", [P, 2 * UNITS])
        RCP = sb("RCP", [P, 2, 8])
        RX = [sb(f"RX{i}", [P, TC, 2, DH]) for i in range(2)]
        RSB = [sb(f"RSB{i}", [P, CH]) for i in range(2)]
        ZN = [sb(f"ZN{i}", [P, CH]) for i in range(2)]
        PT = [sb("PT0", [P, 2, 4, CH]), sb("PT1", [P, 2, 8, CH])]
        NST = PR[3][:, 0:6 * NT].rearrange("p (t c) -> p t c", c=6)
        NMV = PR[3][:, 6 * NT:8 * NT].rearrange("p (t c) -> p t c", c=2)
        NSD, NRS, NVAR, NSD2, NRS2, NSCALE = (PR[3][:, (8 + i) * NT:(9 + i) * NT] for i in range(6))
        NY = [SSB[b % 2][:, :].rearrange("p (t d) -> p t d", d=D) for b in range(B)]
        XST = [XTB[0][:, :], PR[0][:, :], PR[1][:, :], V[1][:, :, :].rearrange("p t d -> p (t d)")]

        LOWER = sb("LOWER", [P, E, E])

        WE1_RAW = XTB[0][:, :].rearrange("p (e h) -> p e h", e=E)
        W2 = XTB[1][:, 0:E * M].rearrange("p (e m) -> p e m", e=E)
        DECW = XTB[1][:, 512:768].rearrange("p (m d) -> p m d", m=HB)
        C2SW = XTB[1][:, 768:1024]
        wv = WV[:, :, :].rearrange("p h e -> p (h e)")
        ENCW = wv[:, 0:256]
        S2CW = wv[:, 256:512].rearrange("p (m c) -> p m c", m=HB)
        DECB = wv[:, 512:640]
        LNG = wv[:, 640:768]
        LNBB = wv[:, 768:896]
        RW1_RAW = wv[:, 896:1024]
        ENCB, S2CB, RB1 = BV[:, 0:2], BV[:, 2:3], BV[:, 3:4]
        RW2, RB2, BE1 = BV[:, 8:16], BV[:, 16:24], BV[:, 24:32]
        C2SB, BE2 = BV[:, 32:34], BV[:, 64:128]
        WE1 = QS[0][:, 0, :].rearrange("p (e h) -> p e h", e=E)
        RW1 = QS[0][:, 1, 0:P]
        HIGH = KL[0][:, 0, :]
        HIGH1 = KL[0][:, 1, 0:P]
        ONES = BV[:, 128:256]
        FST = BV[:, 256:256 + 6 * NT].rearrange("p (t c) -> p t c", c=6)
        FMV = BV[:, 448:448 + 2 * NT].rearrange("p (t c) -> p t c", c=2)
        FSD, FRS = BV[:, 512:512 + NT], BV[:, 544:544 + NT]
        CH_ = [KH[0][:, i, 0:CH] for i in range(2)]
        CL_ = [KH[0][:, i, CH:S] for i in range(2)]
        tiled = lambda f: f.rearrange("p (t d) -> p t d", d=P)
        YF, YT = tiled(RAW[:, 0, :]), RAW[:, 1, :]
        ET = [RH[:, 0, i * CH:(i + 1) * CH].bitcast(F32) for i in range(2)]
        C32, T1 = (RH[:, 1, i * CH:(i + 1) * CH].bitcast(F32) for i in range(2))
        GP = tiled(RL[:, 0, 0:CH].bitcast(F32))
        small = lambda i, n=TC * E: RL[:, 0, CH + i:CH + i + n].bitcast(F32)
        per = lambda x: x.rearrange("p (t e) -> p t e", e=E)
        LG, LM, EX, PB, RK, G1 = (per(small(32 * i)) for i in range(6))
        MX, SUM, RSUM, GS, RG = (small(192 + 4 * i, TC) for i in range(5))
        GR, EQ = (RL[:, 1, 256 * i:256 * i + TC * E * E].bitcast(F32).rearrange("p (t e f) -> p t e f", e=E, f=E) for i in range(2))
        F = [PT[1][:, i // 8, i % 8, :] for i in range(11)]
        H, GH, O, SMT, GT = F[0:2], F[2:6], F[6], F[7:9], F[9]
        DT, DD = tiled(F[10]), tiled(PT[0][:, 0, 0, :])
        NRM, PRO, OUT = tiled(SSB[0][:, 0:CH]), tiled(SSB[0][:, CH:S]), tiled(SSB[1][:, 0:CH])
        ST2, MV2, SD2, RS2 = (sb("ST2", [P, TC, 6]), sb("MV2", [P, TC, 2]), sb("SD2", [P, TC]), sb("RS2", [P, TC]))

        SP_ = [ctx.enter_context(nc.psum_tensor(f"SPS{i}", [P, S], F32)) for i in range(2)]
        TB = [ctx.enter_context(nc.psum_tensor(f"TB{i}", [P, CH], F32)) for i in range(2)]
        Z = ctx.enter_context(nc.psum_tensor("Z", [P, CH], F32))
        MB = ctx.enter_context(nc.psum_tensor("MB", [P, CH], F32))

        GB = [SP_[0][:, 0:CH], SP_[0][:, CH:S]]
        A0, A1 = SP_[1][:, 0:CH], SP_[1][:, CH:S]

        const_loaded = sem("const_loaded"); bqk_loaded = sem("bqk_loaded")
        x_loaded = [sem(f"x_loaded{b}") for b in range(B)]
        scale_set = sem("scale_set")
        mask_step = sem("mask_step")
        pool_const = sem("pool_const")
        ln_loaded = sem("ln_loaded")
        ln_stats = sem("ln_stats"); ln_aggr = sem("ln_aggr"); ln_sd = sem("ln_sd"); ln_step = sem("ln_step")
        ln_y = sem("ln_y")
        xt_turned = sem("xt_turned"); xt_ready = sem("xt_ready"); bo_added = sem("bo_added")
        xt_stored = [sem(f"xt_stored{b}") for b in range(B)]
        staged = [sem(f"staged{i}") for i in range(2)]
        qks_ready = [sem(f"qks_ready{i}") for i in range(2)]
        qks_first = [sem(f"qks_first{c}") for c in range(2)]
        qk_filled = sem("qk_filled"); qk_evac = sem("qk_evac")
        v_filled = sem("v_filled"); v_evac = sem("v_evac")
        rounded = sem("rounded"); split_done = sem("split_done")
        s_filled = sem("s_filled"); s_masked = sem("s_masked"); exp_done = sem("exp_done")
        t_filled = sem("t_filled"); t_copied_act = sem("t_copied_act"); t_copied_dve = sem("t_copied_dve")
        pv_done = sem("pv_done"); zn_done = sem("zn_done")
        rcp_done = sem("rcp_done"); rx_ready = sem("rx_ready")
        r_filled = sem("r_filled"); r_evac = sem("r_evac")
        out_filled = sem("out_filled"); out_evac = sem("out_evac")

        f_loaded = sem("f_loaded"); f_high = sem("f_high"); f_weights = sem("f_weights"); zeroed = sem("zeroed")
        f_sums = sem("f_sums"); f_biases = sem("f_biases")
        f_stats = sem("f_stats"); f_aggr = sem("f_aggr"); f_sd = sem("f_sd"); f_rs = sem("f_rs")
        f_centred = sem("f_centred"); f_y = sem("f_y")
        f_turned = sem("f_turned"); f_yt = sem("f_yt"); f_enc = sem("f_enc"); f_et = sem("f_et")
        f_s2c = sem("f_s2c"); f_c32 = sem("f_c32"); f_cl = sem("f_cl")
        f_r1 = sem("f_r1"); f_t1 = sem("f_t1"); f_lg = sem("f_lg"); gate_step = sem("gate_step"); f_ex = sem("f_ex")
        f_gates = sem("f_gates"); f_gt = sem("f_gt"); f_gtc = sem("f_gtc")
        f_h = sem("f_h"); f_g = sem("f_g"); f_relu = sem("f_relu"); f_gh = sem("f_gh"); f_w2 = sem("f_w2"); f_o = sem("f_o")
        f_c2s = sem("f_c2s"); f_smt = sem("f_smt"); f_dec = sem("f_dec")
        f_d = sem("f_d"); f_dt = sem("f_dt")
        g_stats = sem("g_stats"); g_aggr = sem("g_aggr"); g_sd = sem("g_sd"); g_rs = sem("g_rs"); g_y = sem("g_y")
        nrm_free = sem("nrm_free"); f_shifted = sem("f_shifted"); f_out = sem("f_out"); stored = sem("stored")
        lower_set = sem("lower_set")

        def wait(eng, s, value):
            if not isinstance(value, int) or value > 0:
                eng.wait_ge(s, value)

        block = ctx.enter_context(nc.Block())

        def each_step(eng, body):
            body(0, 0, 0, True, False)
            with eng.Fori(0, STEPS // 2 - 1) as j:
                body(j * 2 + 1, j, 1, False, False)
                body(j * 2 + 2, j + 1, 0, False, False)
            body(STEPS - 1, STEPS // 2 - 1, 1, False, True)

        FNORM = (slice(0, NT - QT), slice(NT - QT, NT))
        NORM_TILES = (slice(0, QT), slice(QT, NT))

        ZN0 = 1
        G6, G7 = 3, 4
        VALUES_0 = {15: (0, 1)}
        PREV_VALUES = {0: [(0, (2, 3))], 4: [(1, (0, 1, 2))], 7: [(1, (3, 4, 5))], 10: [(1, (6, 7))]}

        def turns_of(n):
            t = n // 2
            if n < 8:
                return [(n, 0, t + 1)]
            return [(8 + 2 * (n - 8), 0, 4), (9 + 2 * (n - 8), 4, t - 3)]

        def each_chunk(eng, body):
            body(0, 0, True, False)
            with eng.Fori(0, NC // 2 - 1) as j:
                body(j * 2 + 1, 1, False, False)
                body(j * 2 + 2, 0, False, False)
            body(NC - 1, 1, False, True)

        def spread_count(par, half):
            return (half + (1 if par else 0)) * 96

        def staged_count(par, half):
            return (half + 1) * 64 - (32 if par == 0 else 0)

        FFN_LOADS = 26

        def stage(sp, it, par):
            pair = it % HP
            b = (it // HP) % B
            sp.dma_start(WQK[par][:, :, 0:DH], a["W_q"][bass.ds(pair * 2, 2), :, :].rearrange("h d e -> d h e")).then_inc(staged[par], 16)
            sp.dma_start(WQK[par][:, :, DH:P], a["W_k"][bass.ds(pair * 2, 2), :, :].rearrange("h d e -> d h e")).then_inc(staged[par], 16)
            if not (isinstance(it, int) and it == 0):
                sp.dma_start(BQKS[par][:, :], BQK[:, bass.ds(pair * 2, 2)]).then_inc(staged[par], 16)
                sp.dma_start(XTB[par][:, :], xt_dram[:, bass.ds(b * S, S)]).then_inc(staged[par], 16)

        def spread(sp, it, par):
            sp.wait_ge(split_done, (it + 1) * 4)
            sp.nop(nofuse=True)
            wait(sp, s_filled, (it - 1) * UNITS)
            for dst, src in spread_pairs(par):
                sp.dma_start(dst.bitcast(F32), src.bitcast(F32)).then_inc(qks_ready[par], 16)

        def spread_pairs(par):
            lo, hi = slice(0, DH), slice(DH, P)
            return ((QS[par][lo], RH[lo]), (QS[par][hi], RL[lo]),
                    (KH[par][lo], RH[hi]), (KH[par][hi], RH[hi]),
                    (KL[par][lo], RL[hi]), (KL[par][hi], RL[hi]))

        @block.sync
        def _(sp):
            x_tiles = a["x"].rearrange("b (t p) d -> p (b t) d", p=P)
            def load_x(b):
                sp.dma_start(X[:, b * QT:(b + 1) * QT, :], x_tiles[:, b * QT:(b + 1) * QT, :]).then_inc(x_loaded[b], 16)
            load_x(0)
            sp.dma_start(LNW[:, :], a["ln_w"].rearrange("(d o) -> d o", o=1)).then_inc(ln_loaded, 16)
            sp.dma_start(LNB[:, :], a["ln_b"].rearrange("(d o) -> d o", o=1)).then_inc(ln_loaded, 16)
            sp.dma_start(BQK[0:DH, :], a["b_q"].rearrange("h e -> e h"), allow_slow_non_contiguous=True).then_inc(bqk_loaded, 16)
            sp.dma_start(BQK[DH:P, :], a["b_k"].rearrange("h e -> e h"), allow_slow_non_contiguous=True).then_inc(bqk_loaded, 16)
            stage(sp, 0, 0)
            load_x(1)
            sp.dma_start(WV[:, :, :], a["W_v"].rearrange("h d e -> d h e")).then_inc(const_loaded, 16)
            sp.dma_start(BV[:, :], a["b_v"].rearrange("h e -> (h e)").partition_broadcast(P)).then_inc(const_loaded, 16)
            sp.dma_start(BO[:, :], a["b_o"].partition_broadcast(P)).then_inc(const_loaded, 16)
            load_x(2)
            load_x(3)
            sp.dma_start(WO[:, :, :], a["W_o"].rearrange("(p h) e d -> (h e) p d", h=2)).then_inc(const_loaded, 16)

            def store_xt(b):
                sp.wait_ge(xt_ready, 2 * b + 2)
                sp.dma_start(xt_dram[:, b * S:(b + 1) * S], XST[b]).then_inc(xt_stored[b], 16)
            store_xt(0)
            sp.wait_ge(xt_stored[0], 16)
            sp.wait_ge(pool_const, 3)
            stage(sp, 1, 1)
            for c in range(2):
                sp.wait_ge(split_done, 2 * c + 2)
                for dst, src in spread_pairs(0):
                    part = slice(c * CH, (c + 1) * CH)
                    sp.dma_start(dst[:, :, part].bitcast(F32), src[:, :, part].bitcast(F32)).then_inc(qks_first[c], 16)
            for b in range(1, B):
                store_xt(b)
            for b in range(1, B):
                sp.wait_ge(xt_stored[b], 16)

            def body(it, half, par, first, last):
                if not last:
                    sp.wait_ge(v_filled, (it + 1) * 2)
                    stage(sp, it + 2, par)
                    spread(sp, it + 1, 1 - par)
            each_step(sp, body)
            sp.wait_ge(v_filled, STEPS * 2)
            sp.wait_ge(v_evac, STEPS * 2)
            sp.wait_ge(staged[0], staged_count(0, STEPS // 2))
            sp.wait_ge(zeroed, 1)
            col = lambda x: x.rearrange("(o p) -> p o", o=1)
            n = 0
            for dst, src in [(WE1_RAW[r], a["We1"].rearrange("e m h -> m e h")) for r in (slice(0, M), slice(M, P))] + \
                    [(W2, a["We2"].rearrange("e h m -> h e m")), (DECW, a["dec_W"].rearrange("(m p) d -> p m d", p=P)),
                     (C2SW[0:M], a["c2s_W"]), (C2SW[M:P], a["c2s_W"]), (ENCW, a["enc_W"]),
                     (S2CW[:, :, 0:M], a["s2c_W"].rearrange("(m p) c -> p m c", p=P)),
                     (S2CW[:, :, M:P], a["s2c_W"].rearrange("(m p) c -> p m c", p=P)),
                     (DECB, a["dec_b"].partition_broadcast(P)), (LNG, a["ln_g"].partition_broadcast(P)),
                     (LNBB, a["ln_b2"].partition_broadcast(P)),
                     (RW1_RAW[0:M, 0:M], a["rW1"]), (RW1_RAW[M:P, 0:M], a["rW1"]),
                     (RW1_RAW[0:M, M:P], a["rW1"]), (RW1_RAW[M:P, M:P], a["rW1"]),
                     (S2CB[0:M], col(a["s2c_b"])), (S2CB[M:P], col(a["s2c_b"])),
                     (RB1[0:M], col(a["rb1"])), (RB1[M:P], col(a["rb1"])),
                     (RW2[0:M], a["rW2"]), (RB2, a["rb2"].partition_broadcast(P)),
                     (ENCB, a["enc_b"].rearrange("(m p) -> p m", p=P)), (C2SB, a["c2s_b"].rearrange("(m p) -> p m", p=P)),
                     (BE1, a["be1"].rearrange("e h -> h e")), (BE2[0:E], a["be2"])]:
                sp.dma_start(dst, src, allow_slow_non_contiguous=True).then_inc(f_loaded, 16)
                n += 1
            assert n == FFN_LOADS
            out_tiles = out.rearrange("b (t p) d -> p (b t) d", p=P)

            def store(c):
                sp.wait_ge(f_out, c + 1)
                sp.dma_start(out_tiles[:, bass.ds(c * TC, TC), :], OUT).then_inc(stored, 16)
            with sp.Fori(0, NC) as c:
                store(c)
            sp.wait_ge(stored, NC * 16)

        def expand(gp, it, g):
            gp.wait_ge(rcp_done, it * 2 + g + 1)
            wait(gp, r_filled, it * 2 + (1 if g else -1))
            gp.nop(nofuse=True)
            gp.tensor_copy(RX[g][:, :, :, :], RCP[:, g, :].rearrange("p (t h) -> p t h", h=2).unsqueeze(3).broadcast_to([P, TC, 2, DH])).then_inc(rx_ready, 1)

        def split(gp, it, half_prev, par_prev, parts):
            if isinstance(it, int) and it == 1 and 0 in parts:
                gp.wait_ge(qks_first[0], 96)
                gp.wait_ge(qks_first[1], 96)
            elif half_prev is not None and 0 in parts:
                gp.wait_ge(qks_ready[par_prev], spread_count(par_prev, half_prev))
            for s in parts:
                h, c = s % 2, s // 2
                part = slice(c * CH, (c + 1) * CH)
                gp.wait_ge(qk_evac, it * 4 + s + 1)
                if half_prev is not None:
                    gp.nop(nofuse=True)
                    gp.tensor_copy(RH[:, h, part], RAW[:, s % 2, :]).then_inc(rounded, 1)
                gp.wait_ge(rounded, it * 4 + s + 1)
                gp.tensor_tensor(RL[:, h, part], RAW[:, s % 2, :], RH[:, h, part].bitcast(F32), ALU.subtract).then_inc(split_done, 1)

        @block.gpsimd
        def _(gp):
            gp.memset(IDENT[:, :], 0.0).then_inc(mask_step, 1)
            gp.memset(MASK[:, :], 0.0).then_inc(mask_step, 1)
            gp.wait_ge(mask_step, 2)
            gp.affine_select(out=IDENT[:, :], in_=IDENT[:, :], compare_op=ALU.not_equal, fill=1.0,
                             base=0, pattern=[[-1, P]], channel_multiplier=1).then_inc(pool_const, 1)
            gp.affine_select(out=MASK[:, S - P:S], in_=MASK[:, S - P:S], compare_op=ALU.is_ge, fill=BIG,
                             base=0, pattern=[[-1, P]], channel_multiplier=1).then_inc(pool_const, 1)
            gp.memset(LOWER[:, :, :], 1.0).then_inc(lower_set, 1)
            gp.wait_ge(lower_set, 1)
            gp.affine_select(out=LOWER[:, :, :], in_=LOWER[:, :, :], compare_op=ALU.is_gt, fill=0.0,
                             base=0, pattern=[[1, E], [-1, E]], channel_multiplier=0).then_inc(lower_set, 1)
            gp.wait_ge(bqk_loaded, 32)
            gp.wait_ge(scale_set, 4)
            gp.tensor_scalar(BQK[:, :], BQK[:, :], QKSCALE[:, 0:1], None, ALU.mult).then_inc(pool_const, 1)
            split(gp, 0, None, None, range(4))
            gp.wait_ge(const_loaded, 16 * 4)
            for b in range(B):
                gp.wait_ge(ln_y, 2 * b + 2)
                gp.tensor_tensor(X[:, b * QT:(b + 1) * QT, :], X[:, b * QT:(b + 1) * QT, :],
                                 BO[:, :].unsqueeze(1).broadcast_to([P, QT, D]), ALU.add).then_inc(bo_added, 1)

            def body(it, half, par, first, last):
                if not last:
                    split(gp, it + 1, half, par, (0, 1))
                if not first:
                    expand(gp, it - 1, 1)
                if not last:
                    split(gp, it + 1, half, par, (2, 3))
                expand(gp, it, 0)
            each_step(gp, body)

            def norm_in(c, k):
                wait(gp, f_turned, k)
                gp.tensor_tensor(YF, X[:, bass.ds(c * TC, TC), :],
                                 FMV[:, bass.ds(c * TC, TC), 0:1].broadcast_to([P, TC, D]), ALU.subtract).then_inc(f_centred, 1)
                gp.wait_ge(f_centred, k + 1)
                gp.tensor_tensor(YF, YF, FRS[:, bass.ds(c * TC, TC)].unsqueeze(2).broadcast_to([P, TC, D]), ALU.mult).then_inc(f_y, 1)

            def finish(c):
                gp.wait_ge(g_y, c + 1)
                gp.tensor_tensor(PRO, NRM, LNG.unsqueeze(1).broadcast_to([P, TC, D]), ALU.mult).then_inc(nrm_free, 1)
                gp.wait_ge(nrm_free, c + 2)
                gp.tensor_tensor(OUT, PRO, LNBB.unsqueeze(1).broadcast_to([P, TC, D]), ALU.add).then_inc(f_shifted, 1)
                gp.wait_ge(f_shifted, c + 1)
                gp.tensor_tensor(OUT, OUT, X[:, bass.ds(c * TC, TC), :], ALU.add).then_inc(f_out, 1)
                gp.wait_ge(stored, (c + 1) * 16)
            gp.wait_ge(f_rs, 1)
            norm_in(0, 0)
            expand(gp, STEPS - 1, 1)
            norm_in(1, 1)
            gp.wait_ge(exp_done, STEPS * UNITS)
            gp.memset(PRO[:, 0, 0:1], 0.0).then_inc(nrm_free, 1)

            def chunk(c, par, first, last):
                if not last:
                    norm_in((c + 2) % NC, c + 2)
                if first:
                    gp.wait_ge(f_rs, 2)
                else:
                    finish(c - 1)
            each_chunk(gp, chunk)
            finish(NC - 1)

        def pe_qk(pe, par, s, bank=MB):
            h, c = s % 2, s // 2
            pe.matmul(bank[:, :], WQK[par][:, h, :], XTB[par][:, c * CH:(c + 1) * CH], start=True, stop=True).then_inc(qk_filled, 1)

        def pe_v(pe, it, par, s, bank=MB):
            for k in range(TC):
                t = s * TC + k
                last = pe.matmul(bank[:, k * P:(k + 1) * P], XTB[par][:, t * P:(t + 1) * P],
                                 WV[:, bass.ds((it % HP) * 2, 2), :].rearrange("p h e -> p (h e)"), start=True, stop=True)
            last.then_inc(v_filled, 1)

        def pe_scores(pe, it, par, n):
            t, h = n // 2, n % 2
            w = (t + 1) * P
            for c0 in range(0, w, CH):
                wc = max(min(CH, w - c0), 256)
                pe.matmul(SP_[n % 2][:, c0:c0 + wc], QS[par][:, h, t * P:(t + 1) * P], KH[par][:, h, c0:c0 + wc], start=True, stop=False)
                last = pe.matmul(SP_[n % 2][:, c0:c0 + wc], QS[par][:, h, t * P:(t + 1) * P], KL[par][:, h, c0:c0 + wc], start=False, stop=True)
            last.then_inc(s_filled, 1)

        def pe_turn(pe, it, n):
            pe.wait_ge(exp_done, it * UNITS + n + 1)
            for idx, j0, nb in turns_of(n):
                wait(pe, t_copied_act if idx % 2 == 0 else t_copied_dve, it * HALF_TURNS + idx // 2)
                for k in range(nb):
                    last = pe.transpose(TB[idx % 2][:, k * P:(k + 1) * P], PR[n % 4][:, (j0 + k) * P:(j0 + k + 1) * P], IDENT[:, :])
                last.then_inc(t_filled, 1)

        def pe_values(pe, it, par, g, j):
            if j == 0:
                done = it * HALF_TURNS + (4 if g == 0 else HALF_TURNS)
                pe.wait_ge(t_copied_act, done)
                pe.wait_ge(t_copied_dve, done)
                pe.wait_ge(v_evac, (it + 1) * 2)
                wait(pe, zn_done, it * 2 + g)
            off = (j - g * TC) * P if j >= g * TC else 0
            nj = (g + 1) * TC
            for h in range(2):
                last = pe.matmul(Z[h * DH:(h + 1) * DH, off:CH], V[par][:, j, h * DH:(h + 1) * DH], PT[g][:, h, j, off:CH],
                                 start=(j == 0), stop=(j == nj - 1))
            if j == nj - 1:
                last.then_inc(pv_done, 1)

        def pe_spread_sums(pe, it, g):
            pe.wait_ge(rx_ready, it * 2 + g + 1)
            for i in range(TC):
                last = pe.transpose(MB[:, i * P:(i + 1) * P], RX[g][:, i, :, :].rearrange("p h e -> p (h e)"), IDENT[:, :])
            last.then_inc(r_filled, 1)

        def pe_out(pe, it, g):
            pe.wait_ge(zn_done, it * 2 + g + 1)
            for i in range(TC):
                last = pe.matmul(MB[:, i * P:(i + 1) * P], ZN[g][:, i * P:(i + 1) * P],
                                 WO[:, bass.ds(it % HP, 1), :].rearrange("p o d -> p (o d)"), start=True, stop=True)
            last.then_inc(out_filled, 1)

        def pe_slot(pe, it, half, par, first, last, n):
            if n == 0:
                pe.wait_ge(qks_first[0], 96) if first else pe.wait_ge(qks_ready[par], spread_count(par, half))
            if n == 8 and first:
                pe.wait_ge(qks_first[1], 96)
            wait(pe, s_masked, it * UNITS + n - 1)
            pe_scores(pe, it, par, n)
            if n < 4 and not last:
                if n == 0:
                    pe.wait_ge(v_evac, it * 2 + 2)
                    nhalf = half + 1 if par else half
                    pe.wait_ge(staged[1 - par], staged_count(1 - par, nhalf))
                else:
                    pe.wait_ge(qk_evac, it * 4 + 4 + n)
                pe_qk(pe, 1 - par, n)
            if n == 5 and not first:
                if last:
                    pe.wait_ge(v_evac, it * 2 + 2)
                else:
                    pe.wait_ge(qk_evac, it * 4 + 8)
                pe_out(pe, it - 1, 0)
            if n == 7 and not first:
                pe.wait_ge(out_evac, it * 2 - 1)
                pe_spread_sums(pe, it - 1, 1)
            if n == 12:
                if first:
                    pe.wait_ge(qk_evac, 8)
                else:
                    pe.wait_ge(r_evac, it * 2)
                pe_spread_sums(pe, it, 0)
            if n == 13 and not first:
                pe.wait_ge(r_evac, it * 2 + 1)
                pe_out(pe, it - 1, 1)
            if n in (14, 15) and not last:
                if n == 14 and first:
                    pe.wait_ge(r_evac, 1)
                elif n == 14:
                    pe.wait_ge(out_evac, it * 2)
                else:
                    pe.wait_ge(v_evac, it * 2 + 3)
                pe_v(pe, it + 1, 1 - par, n - 14)
            if n >= 3:
                pe_turn(pe, it, n - 3)
            elif not first:
                pe_turn(pe, it - 1, UNITS + n - 3)
            for g, js in PREV_VALUES.get(n, ()):
                if not first:
                    for j in js:
                        pe_values(pe, it - 1, 1 - par, g, j)
            for j in VALUES_0.get(n, ()):
                pe_values(pe, it, par, 0, j)

        def pe_norm_turn(pe, k):
            pe.wait_ge(f_y, k + 1)
            wait(pe, f_t1, k)
            for i in range(TC):
                last = pe.transpose(A0[:, i * P:(i + 1) * P], YF[:, i, :], IDENT[:, :])
            last.then_inc(f_turned, 1)

        def pe_encode(pe, c):
            pe.wait_ge(f_yt, c + 1)
            wait(pe, gate_step, c * GSTEPS - GSTEPS + 1)
            for m, bank in ((0, A1), (1, A0)):
                pe.matmul(bank, ENCW[:, m * P:(m + 1) * P], YT, start=True, stop=True).then_inc(f_enc, 1)

        def pe_cont(pe, c):
            pe.wait_ge(f_et, c * 2 + 2)
            for m in range(HB):
                last = pe.matmul(A1, S2CW[:, m, :], ET[m], start=(m == 0), stop=(m == HB - 1))
            last.then_inc(f_s2c, 1)

        def pe_router(pe, c, par):
            pe.wait_ge(f_cl, c + 1)
            pe.matmul(A0, RW1, CH_[par], start=True, stop=False)
            pe.matmul(A0, RW1, CL_[par], start=False, stop=True).then_inc(f_r1, 1)

        def pe_logits(pe, c):
            pe.wait_ge(f_t1, c + 1)
            for k in range(TC):
                last = pe.matmul(A1[:, k * E:(k + 1) * E], T1[:, k * P:(k + 1) * P], RW2, start=True, stop=True)
            last.then_inc(f_lg, 1)

        def pe_gate_turn(pe, c):
            wait(pe, f_d, c)
            for k in range(TC):
                last = pe.transpose(MB[:, k * P:(k + 1) * P], GP[:, k, :], IDENT[:, :])
            last.then_inc(f_gt, 1)

        def pe_hidden(pe, c, par, e):
            wait(pe, f_relu, c * E + e - 1)
            pe.matmul(TB[e % 2][:, :], WE1[:, e, :], CH_[par], start=True, stop=False)
            pe.matmul(TB[e % 2][:, :], WE1[:, e, :], CL_[par], start=False, stop=True).then_inc(f_h, 1)

        def pe_gates(pe, c, e):
            if e == 0:
                pe.wait_ge(f_gates, c + 1)
            wait(pe, f_gh, c * E + e - 1)
            for k in range(TC):
                last = pe.transpose(GB[e % 2][:, k * P:(k + 1) * P], GP[:, k, e:e + 1].broadcast_to([P, P]), IDENT[:, :])
            last.then_inc(f_g, 1)

        def pe_experts(pe, c, p):
            pe.wait_ge(f_gh, c * E + 2 * p + 2)
            if p == 0:
                wait(pe, f_o, c)
            for e in (2 * p, 2 * p + 1):
                last = pe.matmul(Z[(e % 2) * M:(e % 2 + 1) * M, :], W2[:, e, :], GH[e % 4], start=(p == 0), stop=(e == E - 1))
            if p == E // 2 - 1:
                pe.wait_ge(f_gtc, c + 1)
                last = pe.matmul(Z[0:M, :], BE2, GT, start=False, stop=True)
            last.then_inc(f_w2, 1)

        def pe_c2s(pe, c, m, bank=MB):
            if m == 0:
                pe.wait_ge(f_o, c + 1)
            elif bank is MB:
                pe.wait_ge(f_smt, c * 2 + 1)
            pe.matmul(bank[:, :], C2SW[:, m * P:(m + 1) * P], O, start=True, stop=True).then_inc(f_c2s, 1)

        def pe_decode(pe, c):
            pe.wait_ge(f_smt, c * 2 + 2)
            for k in range(TC):
                for m in range(HB):
                    last = pe.matmul(MB[:, k * P:(k + 1) * P], SMT[m][:, k * P:(k + 1) * P], DECW[:, m, :], start=(m == 0), stop=(m == HB - 1))
            last.then_inc(f_dec, 1)

        @block.tensor
        def _(pe):
            pe.wait_ge(pool_const, 1)
            def turn_norm(b):
                for r in range(2):
                    pe.wait_ge(ln_y, 2 * b + r + 1)
                    if b >= 2:
                        pe.wait_ge(xt_ready, 2 * (b - 2) + r + 1)
                    for k in range(r * TC, (r + 1) * TC):
                        last = pe.transpose(SP_[b % 2][:, k * P:(k + 1) * P], NY[b][:, k, :], IDENT[:, :])
                    last.then_inc(xt_turned, 1)
            turn_norm(0)
            pe.wait_ge(staged[0], 32)
            for s in range(4):
                pe.wait_ge(xt_ready, 1 + s // 2)
                if s >= 2:
                    pe.wait_ge(rounded, s - 1)
                pe_qk(pe, 0, s, (MB, Z)[s % 2])
            pe.wait_ge(const_loaded, 16 * 4)
            pe.wait_ge(rounded, 4)
            pe_v(pe, 0, 0, 0)
            pe_v(pe, 0, 0, 1, Z)
            turn_norm(1)
            turn_norm(2)
            turn_norm(3)
            pe.wait_ge(xt_ready, 2 * B)

            def body(it, half, par, first, last):
                for n in range(UNITS):
                    pe_slot(pe, it, half, par, first, last, n)
            each_step(pe, body)
            it, par = STEPS - 1, 1
            pe_turn(pe, it, UNITS - 3)
            pe_values(pe, it, par, 0, 2)
            pe_values(pe, it, par, 0, 3)
            pe.wait_ge(s_masked, STEPS * UNITS)
            pe.wait_ge(f_weights, 6)
            pe.matmul(GB[0][:, 0:D], ONES, DECW[:, 0, :], start=True, stop=False)
            pe.matmul(GB[0][:, 0:D], ONES, DECW[:, 1, :], start=False, stop=True)
            pe.matmul(GB[0][:, D:D + 8], S2CW[:, 0, :], ONES[:, 0:8], start=True, stop=False)
            pe.matmul(GB[0][:, D:D + 8], S2CW[:, 1, :], ONES[:, 0:8], start=False, stop=True).then_inc(f_sums, 1)
            pe_norm_turn(pe, 0)
            pe_turn(pe, it, UNITS - 2)
            pe_encode(pe, 0)
            pe_turn(pe, it, UNITS - 1)
            pe.wait_ge(r_evac, STEPS * 2 - 1)
            pe_out(pe, it, 0)
            for j in range(QT // 2):
                pe_values(pe, it, par, 1, j)
            pe_cont(pe, 0)
            for j in range(QT // 2, QT):
                pe_values(pe, it, par, 1, j)
            pe.wait_ge(out_evac, STEPS * 2 - 1)
            pe_spread_sums(pe, STEPS - 1, 1)
            pe_router(pe, 0, 0)
            pe.wait_ge(r_evac, STEPS * 2)
            pe_out(pe, it, 1)
            pe_logits(pe, 0)
            pe_norm_turn(pe, 1)

            pe.wait_ge(t_copied_act, STEPS * HALF_TURNS)
            pe.wait_ge(t_copied_dve, STEPS * HALF_TURNS)
            pe.wait_ge(out_evac, STEPS * 2)
            pe.wait_ge(f_biases, 2)

            def chunk(c, par, first, last):
                for e in (0, 1):
                    pe_hidden(pe, c, par, e)
                if not first:
                    pe_c2s(pe, c - 1, 0)
                if not last:
                    pe_encode(pe, c + 1)
                for e in (0, 1):
                    pe_gates(pe, c, e)
                if not first:
                    pe_c2s(pe, c - 1, 1)
                for e in (2, 3):
                    pe_hidden(pe, c, par, e)
                if not last:
                    pe_cont(pe, c + 1)
                for e in (2, 3):
                    pe_gates(pe, c, e)
                pe_experts(pe, c, 0)
                if not first:
                    pe_decode(pe, c - 1)
                for e in (4, 5):
                    pe_hidden(pe, c, par, e)
                if not last:
                    pe_router(pe, c + 1, 1 - par)
                for e in (4, 5):
                    pe_gates(pe, c, e)
                pe_experts(pe, c, 1)
                if not last:
                    pe_logits(pe, c + 1)
                for e in (6, 7):
                    pe_hidden(pe, c, par, e)
                pe_gate_turn(pe, c)
                for e in (6, 7):
                    pe_gates(pe, c, e)
                pe_experts(pe, c, 2)
                if not last:
                    pe_norm_turn(pe, c + 2)
                pe_experts(pe, c, 3)
            each_chunk(pe, chunk)
            pe_c2s(pe, NC - 1, 0)
            pe_c2s(pe, NC - 1, 1, A0)
            pe_decode(pe, NC - 1)

        def copy_turn(eng, which, it, n):
            t, h = n // 2, n % 2
            g, tq = t // TC, t % TC
            for idx, j0, nb in turns_of(n):
                if idx % 2 == which:
                    eng.wait_ge(t_filled, it * TURNS + idx + 1)
                    dst = PT[g][:, h, j0:j0 + nb, tq * P:(tq + 1) * P]
                    src = TB[idx % 2][:, 0:nb * P].rearrange("p (j q) -> p j q", q=P)
                    if which == 0:
                        eng.activation(dst, src, ACT.Copy).then_inc(t_copied_act, 1)
                    else:
                        eng.tensor_copy(dst, src).then_inc(t_copied_dve, 1)

        def dve_reciprocal(v, it, g, par):
            v.wait_ge(exp_done, it * UNITS + 8 * g + 8)
            wait(v, rx_ready, it * 2 + (1 if g else -1))
            c0 = par * UNITS + g * 8
            v.reciprocal(RCP[:, g, :], L[:, c0:c0 + 8]).then_inc(rcp_done, 1)

        def dve_zn(v, it, g):
            v.wait_ge(pv_done, it * 2 + g + 1)
            v.wait_ge(r_evac, it * 2 + g + 1)
            v.tensor_tensor(ZN[g][:, :], Z[:, :], RSB[g][:, :], ALU.mult).then_inc(zn_done, 1)

        def dve_out(v, it, g):
            v.wait_ge(out_filled, it * 2 + g + 1)
            xs = X[:, bass.ds((it // HP) * QT + g * TC, TC), :]
            v.tensor_tensor(xs, xs, MB[:, :].rearrange("p (t d) -> p t d", d=D), ALU.add).then_inc(out_evac, 1)

        def dve_v(v, it, par, s, bank=MB):
            v.wait_ge(v_filled, it * 2 + s + 1)
            wait(v, pv_done, (it - 1) * 2)
            v.tensor_tensor(V[par][:, s * TC:(s + 1) * TC, :], bank[:, :].rearrange("p (t d) -> p t d", d=P),
                            BV[:, bass.ds((it % HP) * P, P)].unsqueeze(1).broadcast_to([P, TC, P]), ALU.add).then_inc(v_evac, 1)

        def dve_prepare(v, n):
            if n == 0:
                v.wait_ge(f_high, 2)
                v.tensor_tensor(QS[0][M:P, 0, :], XTB[0][M:P, :], HIGH[M:P].bitcast(F32), ALU.subtract).then_inc(f_weights, 1)
            if n == 1:
                v.wait_ge(f_high, 4)
                v.tensor_tensor(RW1[M:P], RW1_RAW[M:P], HIGH1[M:P].bitcast(F32), ALU.subtract).then_inc(f_weights, 1)
                for w in (ENCB, C2SB, S2CW, DECW):
                    v.tensor_scalar(w, w, 0.5, None, ALU.mult).then_inc(f_weights, 1)

        def dve_biases(v):
            v.wait_ge(f_sums, 1)
            v.tensor_tensor(DECB, DECB, GB[0][:, 0:D], ALU.add).then_inc(f_biases, 1)
            v.tensor_tensor(S2CB, S2CB, GB[0][:, D:D + 1], ALU.add).then_inc(f_biases, 1)

        def f_norm_stats(v, tiles):
            for t in tiles:
                v.bn_stats(FST[:, t, :], X[:, t, :]).then_inc(f_stats, 1)
            for t in tiles:
                v.wait_ge(f_stats, t + 1)
                v.bn_aggr(FMV[:, t, :], FST[:, t, :]).then_inc(f_aggr, 1)

        def f_norm_scale(v, i):
            v.wait_ge(f_sd, i + 1)
            v.reciprocal(FRS[:, FNORM[i]], FSD[:, FNORM[i]]).then_inc(f_rs, 1)

        def dve_slot(v, it, half, par, first, last, n):
            w = (n // 2 + 1) * P
            v.wait_ge(s_filled, it * UNITS + n + 1)
            wait(v, exp_done, it * UNITS + n - 1)
            v.nop(nofuse=True)
            v.tensor_tensor_reduce(out=SSB[n % 2][:, 0:w], in0=SP_[n % 2][:, 0:w], in1=MASK[:, S - w:S], scale=1.0, scalar=BIG,
                                   op0=ALU.add, op1=ALU.min, accum_out=NM[:, par * UNITS + n:par * UNITS + n + 1]).then_inc(s_masked, 1)
            if not first:
                if n == ZN0:
                    dve_zn(v, it - 1, 0)
                if n == 1:
                    dve_reciprocal(v, it - 1, 1, 1 - par)
                if n == 5:
                    v.wait_ge(bo_added, B)
                    dve_out(v, it - 1, 0)
                if n == 11:
                    dve_zn(v, it - 1, 1)
                if n == 13:
                    dve_out(v, it - 1, 1)
            if n == 9:
                dve_reciprocal(v, it, 0, par)
            if n == 14 and first:
                v.wait_ge(xt_stored[B - 1], 16)
            if n in (14, 15) and not last:
                dve_v(v, it + 1, 1 - par, n - 14)
            if last and n == 0:
                v.wait_ge(v_evac, STEPS * 2)
                v.memset(BV[:, 0:P], 0.0).then_inc(zeroed, 1)
                v.memset(ONES, 1.0).then_inc(zeroed, 1)
                v.wait_ge(qks_ready[1], spread_count(1, half))
                v.memset(GP, 0.0).then_inc(zeroed, 1)
            if last and n in (12, 14):
                dve_prepare(v, (n - 12) // 2)
            if last and n == 15:
                f_norm_scale(v, 0)
            if n >= 3:
                copy_turn(v, 1, it, n - 3)
            elif not first:
                copy_turn(v, 1, it - 1, UNITS + n - 3)
            if last and 1 <= n <= 8:
                if n == 1:
                    v.wait_ge(out_evac, (STEPS - QT) * 2)
                f_norm_stats(v, range(3 * n - 3, 3 * n))

        def gates_1(v, c):
            v.wait_ge(f_lg, c + 1)
            s = c * GSTEPS
            v.tensor_tensor(LG, per(A1[:, 0:TC * E]), RB2.unsqueeze(1).broadcast_to([P, TC, E]), ALU.add).then_inc(gate_step, 1)
            v.wait_ge(gate_step, s + 1)
            v.tensor_reduce(MX, LG, AXIS_X, ALU.max).then_inc(gate_step, 1)
            v.wait_ge(gate_step, s + 2)
            v.tensor_tensor(LM, LG, MX.unsqueeze(2).broadcast_to([P, TC, E]), ALU.subtract).then_inc(gate_step, 1)

        def gates_2(v, c, beside=()):
            s = c * GSTEPS + 3
            beside = dict(beside)
            over = lambda x: x.unsqueeze(2).broadcast_to([P, TC, E])
            first = PB.unsqueeze(3).broadcast_to([P, TC, E, E])
            other = PB.unsqueeze(2).broadcast_to([P, TC, E, E])

            def step(op, n):
                op.then_inc(gate_step, 1)
                if n in beside:
                    beside[n]()
                v.wait_ge(gate_step, s + n)
            v.wait_ge(f_ex, c + 1)
            step(v.tensor_reduce(SUM, EX, AXIS_X, ALU.add), 1)
            step(v.reciprocal(RSUM, SUM), 2)
            step(v.tensor_tensor(PB, EX, over(RSUM), ALU.mult), 3)
            step(v.tensor_tensor(EQ, other, first, ALU.is_equal), 4)
            step(v.tensor_tensor(EQ, EQ, LOWER[:, :, :].unsqueeze(1).broadcast_to([P, TC, E, E]), ALU.mult), 5)
            step(v.tensor_tensor(GR, other, first, ALU.is_gt), 6)
            step(v.tensor_tensor(GR, GR, EQ, ALU.add), 7)
            step(v.tensor_reduce(RK, GR, AXIS_X, ALU.add), 8)
            step(v.scalar_tensor_tensor(G1, RK, 1.5, PB, ALU.is_lt, ALU.mult), 9)
            step(v.tensor_reduce(GS, G1, AXIS_X, ALU.add), 10)
            step(v.reciprocal(RG, GS), 11)
            wait(v, f_g, c * E)
            v.tensor_tensor(GP[:, :, 0:E], G1, over(RG), ALU.mult).then_inc(f_gates, 1)

        def dve_low(v, c, par):
            v.wait_ge(f_c32, c * 2 + 2)
            v.tensor_tensor(CL_[par], C32, CH_[par].bitcast(F32), ALU.subtract).then_inc(f_cl, 1)

        def dve_gate(v, c, e):
            v.wait_ge(f_relu, c * E + e + 1)
            v.wait_ge(f_g, c * E + e + 1)
            wait(v, f_w2, c * 4 + e // 2 - 1)
            v.tensor_tensor(GH[e % 4], H[e % 2], GB[e % 2], ALU.mult).then_inc(f_gh, 1)

        def dve_decoded(v, c):
            v.wait_ge(f_dec, c + 1)
            v.tensor_tensor(DD, tiled(MB[:, :]), DECB.unsqueeze(1).broadcast_to([P, TC, D]), ALU.add).then_inc(f_d, 1)

        def dve_out_stats(v, c):
            v.wait_ge(f_dt, c + 1)
            for k in range(TC):
                v.bn_stats(ST2[:, k, :], DT[:, k, :]).then_inc(g_stats, 1)
            for k in range(TC):
                v.wait_ge(g_stats, c * TC + k + 1)
                v.nop(nofuse=True)
                v.bn_aggr(MV2[:, k, :], ST2[:, k, :]).then_inc(g_aggr, 1)

        def dve_out_norm(v, c):
            v.wait_ge(g_sd, c + 1)
            v.reciprocal(RS2[:, :], SD2[:, :]).then_inc(g_rs, 1)
            v.wait_ge(g_rs, c + 1)
            v.wait_ge(nrm_free, c + 1)
            for k in range(TC):
                last = v.tensor_scalar(NRM[:, k, :], DT[:, k, :], MV2[:, k, 0:1], RS2[:, k:k + 1], ALU.subtract, ALU.mult)
            last.then_inc(g_y, 1)

        @block.vector
        def _(v):
            v.memset(QKSCALE[0:DH, :], -(DH ** -0.5)).then_inc(scale_set, 1)
            v.memset(QKSCALE[DH:P, :], 1.0).then_inc(scale_set, 1)
            v.memset(EPST[:, :], EPS).then_inc(scale_set, 1)
            v.memset(EPS4[:, :], 4 * EPS).then_inc(scale_set, 1)

            def norm_stats(b):
                v.wait_ge(x_loaded[b], 16)
                for k in range(b * QT, (b + 1) * QT):
                    v.bn_stats(NST[:, k, :], X[:, k, :]).then_inc(ln_stats, 1)
                for k in range(b * QT, (b + 1) * QT):
                    v.wait_ge(ln_stats, k + 1)
                    v.bn_aggr(NMV[:, k, :], NST[:, k, :]).then_inc(ln_aggr, 1)

            def norm_scale(i, t):
                def step(op, n):
                    op.then_inc(ln_step, 1)
                    v.wait_ge(ln_step, i * 5 + n)
                v.wait_ge(ln_sd, 2 * i + 1)
                step(v.reciprocal(NRS[:, t], NSD[:, t]), 1)
                step(v.tensor_tensor(NVAR[:, t], NMV[:, t, 1], NRS[:, t], ALU.mult), 2)
                v.tensor_tensor(NVAR[:, t], NVAR[:, t], NRS[:, t], ALU.mult).then_inc(ln_step, 1)
                v.wait_ge(ln_sd, 2 * i + 2)
                step(v.reciprocal(NRS2[:, t], NSD2[:, t]), 4)
                step(v.tensor_tensor(NSCALE[:, t], NRS[:, t], NRS2[:, t], ALU.mult), 5)

            def norm_apply(b):
                if b >= 2:
                    v.wait_ge(xt_turned, 2 * (b - 1))
                for k in range(QT):
                    t = b * QT + k
                    op = v.tensor_scalar(NY[b][:, k, :], X[:, t, :], NMV[:, t, 0:1], NSCALE[:, t:t + 1], ALU.subtract, ALU.mult)
                    if k % TC == TC - 1:
                        op.then_inc(ln_y, 1)
            norm_stats(0)
            norm_scale(0, NORM_TILES[0])
            norm_apply(0)
            for b in range(1, B):
                norm_stats(b)
            norm_scale(1, NORM_TILES[1])
            v.wait_ge(const_loaded, 16 * 4)
            norm_apply(1)
            dve_v(v, 0, 0, 0)
            dve_v(v, 0, 0, 1, Z)
            norm_apply(2)
            norm_apply(3)
            v.wait_ge(pool_const, 2)

            def body(it, half, par, first, last):
                for n in range(UNITS):
                    dve_slot(v, it, half, par, first, last, n)
            each_step(v, body)
            it = STEPS - 1
            dve_zn(v, it, 0)
            for n in range(3):
                copy_turn(v, 1, it, UNITS + n - 3)
            dve_reciprocal(v, it, 1, 1)
            dve_out(v, it, 0)
            dve_biases(v)
            v.wait_ge(out_evac, STEPS * 2 - 1)
            f_norm_stats(v, range(NT - QT, NT - TC))
            v.wait_ge(zeroed, 3)
            dve_low(v, 0, 0)
            dve_zn(v, it, 1)
            dve_out(v, it, 1)
            gates_1(v, 0)
            gates_2(v, 0)

            def chunk(c, par, first, last):
                for e in range(4):
                    dve_gate(v, c, e)
                if not last:
                    dve_low(v, c + 1, 1 - par)
                if not first:
                    dve_decoded(v, c - 1)
                dve_gate(v, c, 4)
                dve_gate(v, c, 5)
                if first:
                    v.wait_ge(out_evac, STEPS * 2)
                    f_norm_stats(v, range(NT - TC, NT))
                else:
                    dve_out_stats(v, c - 1)
                if not last:
                    gates_1(v, c + 1)
                    gates_2(v, c + 1, [(G6, lambda: dve_gate(v, c, 6)), (G7, lambda: dve_gate(v, c, 7))])
                else:
                    dve_gate(v, c, 6)
                    dve_gate(v, c, 7)
                if first:
                    f_norm_scale(v, 1)
                else:
                    dve_out_norm(v, c - 1)
            each_chunk(v, chunk)
            dve_decoded(v, NC - 1)
            dve_out_stats(v, NC - 1)
            dve_out_norm(v, NC - 1)

        def act_qk(act, it, s, bias, bank=MB):
            h, c = s % 2, s // 2
            act.wait_ge(qk_filled, it * 4 + s + 1)
            wait(act, split_done, it * 4 + s - 1)
            act.activation(RAW[:, s % 2, :], bank[:, :], ACT.Identity, bias=bias[:, h:h + 1], scale=QKSCALE[:, 0:1]).then_inc(qk_evac, 1)

        def act_sums(act, it, g):
            act.wait_ge(r_filled, it * 2 + g + 1)
            wait(act, zn_done, it * 2 + (1 if g else -1))
            act.activation(RSB[g][:, :], MB[:, :], ACT.Copy).then_inc(r_evac, 1)

        def weight_halves(act, r):
            act.wait_ge(f_loaded, FFN_LOADS * 16)
            raw, high, stack = ((XTB[0][:, :], HIGH, QS[0][:, 0, :]), (RW1_RAW, HIGH1, RW1))[r // 2]
            if r % 2 == 0:
                act.activation(high, raw, ACT.Copy).then_inc(f_high, 1)
            else:
                act.activation(stack[0:M], raw[0:M], ACT.Copy).then_inc(f_high, 1)

        def f_deviations(act, i):
            act.wait_ge(f_aggr, FNORM[i].stop)
            act.activation(FSD[:, FNORM[i]], FMV[:, FNORM[i], 1], ACT.Sqrt, bias=EPST[:, 0:1]).then_inc(f_sd, 1)

        def act_slot(act, it, half, par, first, last, n):
            if n < 4 and not last:
                act_qk(act, it + 1, n, BQKS[1 - par])
            if n == 7 and not first:
                act_sums(act, it - 1, 1)
            if n == 12:
                act_sums(act, it, 0)
            if last and 9 <= n <= 11:
                weight_halves(act, n - 9)
            if last and n == 12:
                weight_halves(act, 3)
            if last and n == 14:
                f_deviations(act, 0)
            if n >= 3:
                copy_turn(act, 0, it, n - 3)
            elif not first:
                copy_turn(act, 0, it - 1, UNITS + n - 3)
            w = (n // 2 + 1) * P
            col = par * UNITS + n
            act.wait_ge(s_masked, it * UNITS + n + 1)
            if n >= 4:
                act.wait_ge(t_filled, it * TURNS + turns_of(n - 4)[-1][0] + 1)
            elif not first:
                act.wait_ge(t_filled, (it - 1) * TURNS + turns_of(UNITS + n - 4)[-1][0] + 1)
            act.activation(PR[n % 4][:, 0:w], SSB[n % 2][:, 0:w], ACT.Exp, bias=NM[:, col:col + 1], scale=-1.0,
                           accum_out=L[:, col:col + 1]).then_inc(exp_done, 1)

        @block.scalar
        def _(act):
            act.wait_ge(scale_set, 4)

            def norm_deviations(i, t):
                act.wait_ge(ln_aggr, t.stop)
                act.activation(NSD[:, t], NMV[:, t, 1], ACT.Sqrt, bias=EPST[:, 0:1]).then_inc(ln_sd, 1)
                act.wait_ge(ln_step, i * 5 + 3)
                act.activation(NSD2[:, t], NVAR[:, t], ACT.Sqrt, bias=EPST[:, 0:1]).then_inc(ln_sd, 1)

            def norm_out(b):
                for r in range(2):
                    act.wait_ge(xt_turned, 2 * b + r + 1)
                    act.activation(XST[b][:, r * CH:(r + 1) * CH], SP_[b % 2][:, r * CH:(r + 1) * CH], ACT.Identity,
                                   bias=LNB[:, 0:1], scale=LNW[:, 0:1]).then_inc(xt_ready, 1)
            norm_deviations(0, NORM_TILES[0])
            act.wait_ge(ln_loaded, 32)
            norm_out(0)
            act.wait_ge(pool_const, 3)
            for s in range(4):
                act_qk(act, 0, s, BQK, (MB, Z)[s % 2])
                act.activation(RH[:, s % 2, (s // 2) * CH:(s // 2 + 1) * CH], (MB, Z)[s % 2][:, :], ACT.Identity,
                               bias=BQK[:, s % 2:s % 2 + 1], scale=QKSCALE[:, 0:1]).then_inc(rounded, 1)
                if s == 1:
                    norm_deviations(1, NORM_TILES[1])
            for b in range(1, B):
                norm_out(b)
            act.wait_ge(xt_stored[1], 16)
            act.wait_ge(xt_stored[2], 16)

            def body(it, half, par, first, last):
                for n in range(UNITS):
                    act_slot(act, it, half, par, first, last, n)
            each_step(act, body)
            it = STEPS - 1
            copy_turn(act, 0, it, UNITS - 3)

            def turned(k):
                act.wait_ge(f_turned, k + 1)
                act.activation(YT, A0, ACT.Copy).then_inc(f_yt, 1)

            def encoded(c):
                for m, bank in ((0, A1), (1, A0)):
                    act.wait_ge(f_enc, c * 2 + m + 1)
                    act.activation(ET[m], bank, ACT.Tanh, bias=ENCB[:, m:m + 1], scale=0.5).then_inc(f_et, 1)

            def cont(c, par):
                act.wait_ge(f_s2c, c + 1)
                wait(act, f_cl, c)
                act.activation(C32, A1, ACT.Identity, bias=S2CB).then_inc(f_c32, 1)
                act.activation(CH_[par], A1, ACT.Identity, bias=S2CB).then_inc(f_c32, 1)

            def routed(c):
                act.wait_ge(f_r1, c + 1)
                act.activation(T1, A0, ACT.Tanh, bias=RB1).then_inc(f_t1, 1)

            def exps(c):
                act.wait_ge(gate_step, c * GSTEPS + 3)
                act.activation(EX, LM, ACT.Exp).then_inc(f_ex, 1)

            def gates_turned(c):
                act.wait_ge(f_gt, c + 1)
                act.activation(GT, MB[:, :], ACT.Copy).then_inc(f_gtc, 1)

            def hidden(c, e):
                act.wait_ge(f_h, c * E + e + 1)
                wait(act, f_gh, c * E + e - 1)
                act.activation(H[e % 2], TB[e % 2][:, :], ACT.Relu, bias=BE1[:, e:e + 1]).then_inc(f_relu, 1)

            def experts(c):
                act.wait_ge(f_w2, c * 4 + 4)
                act.activation(O, Z[:, :], ACT.Copy).then_inc(f_o, 1)

            def out_hidden(c, m, bank=MB):
                act.wait_ge(f_c2s, c * 2 + m + 1)
                act.activation(SMT[m], bank[:, :], ACT.Tanh, bias=C2SB[:, m:m + 1], scale=0.5).then_inc(f_smt, 1)

            def decoded(c):
                act.wait_ge(f_d, c + 1)
                act.activation(DT, DD, ACT.Tanh, scale=0.5).then_inc(f_dt, 1)

            def out_deviation(c):
                act.wait_ge(g_aggr, (c + 1) * TC)
                act.activation(SD2[:, :], MV2[:, :, 1], ACT.Sqrt, bias=EPS4[:, 0:1]).then_inc(g_sd, 1)

            act.wait_ge(f_weights, 6)
            turned(0)
            copy_turn(act, 0, it, UNITS - 2)
            copy_turn(act, 0, it, UNITS - 1)
            encoded(0)
            act.wait_ge(f_biases, 2)
            cont(0, 0)
            act_sums(act, it, 1)
            routed(0)
            turned(1)
            exps(0)

            def chunk(c, par, first, last):
                hidden(c, 0)
                hidden(c, 1)
                if not first:
                    out_hidden(c - 1, 0)
                if not last:
                    encoded(c + 1)
                if not first:
                    out_hidden(c - 1, 1)
                hidden(c, 2)
                hidden(c, 3)
                if not last:
                    cont(c + 1, 1 - par)
                hidden(c, 4)
                hidden(c, 5)
                if not first:
                    decoded(c - 1)
                if not last:
                    routed(c + 1)
                hidden(c, 6)
                if not last:
                    exps(c + 1)
                hidden(c, 7)
                gates_turned(c)
                if first:
                    f_deviations(act, 1)
                else:
                    out_deviation(c - 1)
                if not last:
                    turned(c + 2)
                experts(c)
            each_chunk(act, chunk)
            out_hidden(NC - 1, 0)
            out_hidden(NC - 1, 1, A0)
            decoded(NC - 1)
            out_deviation(NC - 1)


_NAMES = {
    "x": "L0_attn_resid_stream", "W_q": "L0_attn_W_q", "W_k": "L0_attn_W_k", "W_v": "L0_attn_W_v", "W_o": "L0_attn_W_o",
    "b_q": "L0_attn_b_q", "b_k": "L0_attn_b_k", "b_v": "L0_attn_b_v", "b_o": "L0_attn_b_o", "ln_w": "L0_attn_ln_w",
    "ln_b": "L0_attn_ln_b", "enc_W": "L0_ffn_enc_W", "enc_b": "L0_ffn_enc_b", "s2c_W": "L0_ffn_s2c_W", "s2c_b": "L0_ffn_s2c_b",
    "rW1": "L0_ffn_rW1", "rb1": "L0_ffn_rb1", "rW2": "L0_ffn_rW2", "rb2": "L0_ffn_rb2", "We1": "L0_ffn_We1", "be1": "L0_ffn_be1",
    "We2": "L0_ffn_We2", "be2": "L0_ffn_be2", "c2s_W": "L0_ffn_c2s_W", "c2s_b": "L0_ffn_c2s_b", "dec_W": "L0_ffn_dec_W",
    "dec_b": "L0_ffn_dec_b", "ln_g": "L0_ffn_ln_g", "ln_b2": "L0_ffn_ln_b",
}


def kernel(**inputs):
    import concourse.bacc as bacc
    from concourse.bass_utils import run_bass_kernel_spmd

    nc = bacc.Bacc("TRN2", target_bir_lowering=False, num_devices=1)
    arrays, args = {}, {}
    for short, name in _NAMES.items():
        arr = np.ascontiguousarray(inputs[name])
        arrays[f"in_{short}"] = arr
        args[short] = nc.dram_tensor(f"in_{short}", arr.shape, mybir.dt.from_np(arr.dtype), kind="ExternalInput").ap()
    out = nc.dram_tensor("out_x", (B, S, D), F32, kind="ExternalOutput").ap()
    build_program(nc, args, out)
    r = run_bass_kernel_spmd(nc, [arrays], core_ids=[0])
    return r.results[0]["out_x"]
```

```python
from contextlib import ExitStack

import numpy as np
import concourse.bass as bass
from concourse import mybir

F32 = mybir.dt.float32
F32R = mybir.dt.float32r
ACT = mybir.ActivationFunctionType
ALU = mybir.AluOpType
AXIS_X = mybir.AxisListType.X

P = 128
B, S, D = 4, 1024, 128
NH, DH = 16, 64
HP = NH // 2
STEPS = B * HP
QT = S // P
UNITS = 2 * QT
NT = B * S // P
CH = 512
NC = B * S // CH
TC = CH // P
HID, M, E = 256, 64, 8
HB = HID // P
LOW = 32
EPS = 1e-5
GSTEPS = 14
DMA = 16
SPREADS = 6
BIG = 3.0e38
TURNS = 8 + 16
HALF_TURNS = TURNS // 2


def build_program(nc, a, out):
    with ExitStack() as ctx:
        def sb(name, shape, dt=F32):
            return ctx.enter_context(nc.sbuf_tensor(name, shape, dt))

        def sem(name):
            return ctx.enter_context(nc.semaphore(name))

        X = sb("X", [P, NT, D])
        xt_dram = nc.dram_tensor("xt_scratch", (P, B * S), F32, kind="Internal").ap()
        IDENT = sb("IDENT", [P, P])
        MASK = sb("MASK", [P, S])
        WO = sb("WO", [P, HP, D])
        WV = sb("WV", [P, NH, DH])
        BV = sb("BV", [P, NH * DH])
        BO = sb("BO", [P, D])
        BQK = sb("BQK", [P, NH])
        BQKS = [sb(f"BQKS{i}", [P, 2]) for i in range(2)]
        QKSCALE = sb("QKSCALE", [P, 1])
        LNW = sb("LNW", [P, 1])
        LNB = sb("LNB", [P, 1])
        EPST = sb("EPST", [P, 1])
        EPS4 = sb("EPS4", [P, 1])
        WQK = [sb(f"WQK{i}", [P, 2, P]) for i in range(2)]
        XTB = [sb(f"XTB{i}", [P, S]) for i in range(2)]
        RAW = sb("RAW", [P, 2, CH])
        RH = sb("RH", [P, 2, S], F32R)
        RL = sb("RL", [P, 2, S], F32R)
        QS = [sb(f"QS{i}", [P, 2, S], F32R) for i in range(2)]
        KH = [sb(f"KH{i}", [P, 2, S], F32R) for i in range(2)]
        KL = [sb(f"KL{i}", [P, 2, S], F32R) for i in range(2)]
        V = [sb(f"V{i}", [P, QT, P]) for i in range(2)]
        SSB = [sb(f"SSB{i}", [P, S]) for i in range(2)]
        PR = [sb(f"PR{i}", [P, S]) for i in range(4)]
        NM = sb("NM", [P, 2 * UNITS])
        L = sb("L", [P, 2 * UNITS])
        RCP = sb("RCP", [P, 2, 8])
        RX = [sb(f"RX{i}", [P, TC, 2, DH]) for i in range(2)]
        RSB = [sb(f"RSB{i}", [P, CH]) for i in range(2)]
        ZN = [sb(f"ZN{i}", [P, CH]) for i in range(2)]
        PT = [sb("PT0", [P, 2, 4, CH]), sb("PT1", [P, 2, 8, CH])]
        NST = PR[3][:, 0:6 * NT].rearrange("p (t c) -> p t c", c=6)
        NMV = PR[3][:, 6 * NT:8 * NT].rearrange("p (t c) -> p t c", c=2)
        NSD, NRS, NVAR, NSD2, NRS2, NSCALE = (PR[3][:, (8 + i) * NT:(9 + i) * NT] for i in range(6))
        NY = [t[:, :].rearrange("p (t d) -> p t d", d=D) for t in (SSB[0], SSB[1], SSB[0], PR[2])]
        XST = [XTB[0][:, :]] + [PT[1][:, 0, 2 * i:2 * i + 2, :].rearrange("p j q -> p (j q)") for i in range(B - 1)]

        LOWER = sb("LOWER", [P, E, E])

        WE1_RAW = XTB[0][:, :].rearrange("p (e h) -> p e h", e=E)
        W2 = XTB[1][:, 0:E * M].rearrange("p (e m) -> p e m", e=E)
        DECW = XTB[1][:, 512:768].rearrange("p (m d) -> p m d", m=HB)
        C2SW = XTB[1][:, 768:1024]
        wv = WV[:, :, :].rearrange("p h e -> p (h e)")
        ENCW = wv[:, 0:256]
        S2CW = wv[:, 256:512].rearrange("p (m c) -> p m c", m=HB)
        DECB = wv[:, 512:640]
        LNG = wv[:, 640:768]
        LNBB = wv[:, 768:896]
        RW1_RAW = wv[:, 896:1024]
        ENCB, S2CB, RB1 = BV[:, 0:2], BV[:, 2:3], BV[:, 3:4]
        RW2, RB2, BE1 = BV[:, 8:16], BV[:, 16:24], BV[:, 24:32]
        C2SB, BE2 = BV[:, 32:34], BV[:, 64:128]
        WE1 = QS[0][:, 0, :].rearrange("p (e h) -> p e h", e=E)
        RW1 = QS[0][:, 1, 0:P]
        BE2H, BE2L = QS[0][:, 1, P:P + M], QS[0][:, 1, P + M:P + 2 * M]
        SPREAD = KL[0][:, 0, :].rearrange("p (e m) -> p e m", e=E)
        GSTACK = KL[0][:, 1, P:P + CH]
        HIGH = KL[0][:, 0, :]
        HIGH1 = KL[0][:, 1, 0:P]
        ONES = BV[:, 128:256]
        FST = BV[:, 256:256 + 6 * NT].rearrange("p (t c) -> p t c", c=6)
        FMV = BV[:, 448:448 + 2 * NT].rearrange("p (t c) -> p t c", c=2)
        FSD, FRS = BV[:, 512:512 + NT], BV[:, 544:544 + NT]
        CH_ = [KH[0][:, i, 0:CH] for i in range(2)]
        CL_ = [KH[0][:, i, CH:S] for i in range(2)]
        tiled = lambda f: f.rearrange("p (t d) -> p t d", d=P)
        YF, YT = tiled(RAW[:, 0, :]), RAW[:, 1, :]
        ET = [RH[:, 0, i * CH:(i + 1) * CH].bitcast(F32) for i in range(2)]
        C32, T1 = (RH[:, 1, i * CH:(i + 1) * CH].bitcast(F32) for i in range(2))
        GP = tiled(RL[:, 0, 0:CH].bitcast(F32))
        small = lambda i, n=TC * E: RL[:, 0, CH + i:CH + i + n].bitcast(F32)
        twice = lambda x: x[:, :, 0:2 * LOW].rearrange("p t (r e) -> p t r e", r=2)[:, :, :, 0:E]
        per = lambda x: x.rearrange("p (t e) -> p t e", e=E)
        LG, LM, EX, PB, RK, G1 = (per(small(32 * i)) for i in range(6))
        MX, SUM, RSUM, GS, RG = (small(192 + 4 * i, TC) for i in range(5))
        GR, EQ = (RL[:, 1, 256 * i:256 * i + TC * E * E].bitcast(F32).rearrange("p (t e f) -> p t e f", e=E, f=E) for i in range(2))
        F = [PT[1][:, i // 8, i % 8, :] for i in range(11)]
        H, GH, O, SMT = F[0:2], F[2:6], F[6], F[7:9]
        DT, DD = tiled(F[10]), tiled(PT[0][:, 0, 0, :])
        NRM, PRO, OUT = tiled(SSB[0][:, 0:CH]), tiled(SSB[0][:, CH:S]), tiled(SSB[1][:, 0:CH])
        ST2, MV2, SD2, RS2 = (sb("ST2", [P, TC, 6]), sb("MV2", [P, TC, 2]), sb("SD2", [P, TC]), sb("RS2", [P, TC]))

        SP_ = [ctx.enter_context(nc.psum_tensor(f"SPS{i}", [P, S], F32)) for i in range(2)]
        TB = [ctx.enter_context(nc.psum_tensor(f"TB{i}", [P, CH], F32)) for i in range(2)]
        Z = ctx.enter_context(nc.psum_tensor("Z", [P, CH], F32))
        MB = ctx.enter_context(nc.psum_tensor("MB", [P, CH], F32))

        NB = [(SP_[0][:, 0:CH], SP_[0][:, CH:S]), (SP_[1][:, 0:CH], SP_[1][:, CH:S])]
        NB += [NB[0], (TB[0][:, :], TB[1][:, :])]

        GB = [SP_[0][:, 0:CH], SP_[0][:, CH:S]]
        A0, A1 = SP_[1][:, 0:CH], SP_[1][:, CH:S]

        const_loaded = sem("const_loaded"); bqk_loaded = sem("bqk_loaded")
        x_loaded = [sem(f"x_loaded{b}") for b in range(B)]
        scale_set = sem("scale_set")
        mask_step = sem("mask_step")
        pool_const = sem("pool_const")
        ln_loaded = sem("ln_loaded")
        ln_stats = sem("ln_stats"); ln_aggr = sem("ln_aggr"); ln_sd = sem("ln_sd"); ln_step = sem("ln_step")
        ln_y = sem("ln_y")
        xt_turned = sem("xt_turned"); xt_ready = sem("xt_ready"); bo_added = sem("bo_added")
        xt_stored = [sem(f"xt_stored{b}") for b in range(B)]
        staged = [sem(f"staged{i}") for i in range(2)]
        qks_ready = [sem(f"qks_ready{i}") for i in range(2)]
        qks_first = [sem(f"qks_first{c}") for c in range(2)]
        qk_filled = sem("qk_filled"); qk_evac = sem("qk_evac")
        v_filled = sem("v_filled"); v_evac = sem("v_evac")
        rounded = sem("rounded"); split_done = sem("split_done")
        s_filled = sem("s_filled"); s_masked = sem("s_masked"); exp_done = sem("exp_done")
        t_filled = sem("t_filled"); t_copied_act = sem("t_copied_act"); t_copied_dve = sem("t_copied_dve")
        pv_done = sem("pv_done"); zn_done = sem("zn_done")
        rcp_done = sem("rcp_done"); rx_ready = sem("rx_ready")
        r_filled = sem("r_filled"); r_evac = sem("r_evac")
        out_filled = sem("out_filled"); out_evac = sem("out_evac")

        f_loaded = sem("f_loaded"); f_high = sem("f_high"); f_weights = sem("f_weights"); zeroed = sem("zeroed")
        f_sums = sem("f_sums"); f_biases = sem("f_biases")
        f_stats = sem("f_stats"); f_aggr = sem("f_aggr"); f_sd = sem("f_sd"); f_rs = sem("f_rs")
        f_centred = sem("f_centred"); f_y = sem("f_y")
        f_turned = sem("f_turned"); f_yt = sem("f_yt"); f_enc = sem("f_enc"); f_et = sem("f_et")
        f_s2c = sem("f_s2c"); f_c32 = sem("f_c32"); f_cl = sem("f_cl")
        f_r1 = sem("f_r1"); f_t1 = sem("f_t1"); f_lg = sem("f_lg"); gate_step = sem("gate_step"); f_ex = sem("f_ex")
        f_gates = sem("f_gates"); f_gt = sem("f_gt"); f_ghigh = sem("f_ghigh"); f_glow = sem("f_glow"); f_spread = sem("f_spread")
        f_h = sem("f_h"); f_g = sem("f_g"); f_relu = sem("f_relu"); f_gh = sem("f_gh"); f_w2 = sem("f_w2"); f_o = sem("f_o")
        f_c2s = sem("f_c2s"); f_smt = sem("f_smt"); f_dec = sem("f_dec")
        f_d = sem("f_d"); f_dt = sem("f_dt")
        g_stats = sem("g_stats"); g_aggr = sem("g_aggr"); g_sd = sem("g_sd"); g_rs = sem("g_rs"); g_y = sem("g_y")
        nrm_free = sem("nrm_free"); f_shifted = sem("f_shifted"); f_out = sem("f_out"); stored = sem("stored")
        lower_set = sem("lower_set")

        def wait(eng, s, value):
            if not isinstance(value, int) or value > 0:
                eng.wait_ge(s, value)

        block = ctx.enter_context(nc.Block())

        def each_step(eng, body):
            body(0, 0, 0, True, False)
            with eng.Fori(0, STEPS // 2 - 1) as j:
                body(j * 2 + 1, j, 1, False, False)
                body(j * 2 + 2, j + 1, 0, False, False)
            body(STEPS - 1, STEPS // 2 - 1, 1, False, True)

        FNORM = (slice(0, NT - QT), slice(NT - QT, NT))
        NORM_TILES = (slice(0, QT), slice(QT, NT))

        VALUES = {15: (0, 1)}
        VALUES_BEFORE = {0: (0, (2, 3)), 4: (1, (0, 1, 2)), 7: (1, (3, 4, 5)), 10: (1, (6, 7))}

        def turns_of(n):
            t = n // 2
            if n < 8:
                return [(n, 0, t + 1)]
            return [(8 + 2 * (n - 8), 0, 4), (9 + 2 * (n - 8), 4, t - 3)]

        def each_chunk(eng, body):
            body(0, 0, True, False)
            with eng.Fori(0, NC // 2 - 1) as j:
                body(j * 2 + 1, 1, False, False)
                body(j * 2 + 2, 0, False, False)
            body(NC - 1, 1, False, True)

        def spread_count(par, half):
            return (half + (1 if par else 0)) * SPREADS * DMA

        def staged_count(par, half):
            return ((half + 1) * 4 - (2 if par == 0 else 0)) * DMA

        FFN_LOADS = 27

        def stage(sp, it, par):
            pair = it % HP
            b = (it // HP) % B
            sp.dma_start(WQK[par][:, :, 0:DH], a["W_q"][bass.ds(pair * 2, 2), :, :].rearrange("h d e -> d h e")).then_inc(staged[par], DMA)
            sp.dma_start(WQK[par][:, :, DH:P], a["W_k"][bass.ds(pair * 2, 2), :, :].rearrange("h d e -> d h e")).then_inc(staged[par], DMA)
            if not (isinstance(it, int) and it == 0):
                sp.dma_start(BQKS[par][:, :], BQK[:, bass.ds(pair * 2, 2)]).then_inc(staged[par], DMA)
                sp.dma_start(XTB[par][:, :], xt_dram[:, bass.ds(b * S, S)]).then_inc(staged[par], DMA)

        def spread(sp, it, par):
            sp.wait_ge(split_done, (it + 1) * 4)
            sp.nop(nofuse=True)
            wait(sp, s_filled, (it - 1) * UNITS)
            for dst, src in spread_pairs(par):
                sp.dma_start(dst.bitcast(F32), src.bitcast(F32)).then_inc(qks_ready[par], DMA)

        def spread_pairs(par):
            lo, hi = slice(0, DH), slice(DH, P)
            return ((QS[par][lo], RH[lo]), (QS[par][hi], RL[lo]),
                    (KH[par][lo], RH[hi]), (KH[par][hi], RH[hi]),
                    (KL[par][lo], RL[hi]), (KL[par][hi], RL[hi]))

        @block.sync
        def _(sp):
            x_tiles = a["x"].rearrange("b (t p) d -> p (b t) d", p=P)

            def load_x(b):
                sp.dma_start(X[:, b * QT:(b + 1) * QT, :], x_tiles[:, b * QT:(b + 1) * QT, :]).then_inc(x_loaded[b], DMA)
            load_x(0)
            sp.dma_start(LNW[:, :], a["ln_w"].rearrange("(d o) -> d o", o=1)).then_inc(ln_loaded, DMA)
            sp.dma_start(LNB[:, :], a["ln_b"].rearrange("(d o) -> d o", o=1)).then_inc(ln_loaded, DMA)
            sp.dma_start(BQK[0:DH, :], a["b_q"].rearrange("h e -> e h"), allow_slow_non_contiguous=True).then_inc(bqk_loaded, DMA)
            sp.dma_start(BQK[DH:P, :], a["b_k"].rearrange("h e -> e h"), allow_slow_non_contiguous=True).then_inc(bqk_loaded, DMA)
            stage(sp, 0, 0)
            load_x(1)
            sp.dma_start(WV[:, :, :], a["W_v"].rearrange("h d e -> d h e")).then_inc(const_loaded, DMA)
            sp.dma_start(BV[:, :], a["b_v"].rearrange("h e -> (h e)").partition_broadcast(P)).then_inc(const_loaded, DMA)
            sp.dma_start(BO[:, :], a["b_o"].partition_broadcast(P)).then_inc(const_loaded, DMA)
            load_x(2)
            load_x(3)
            sp.dma_start(WO[:, :, :], a["W_o"].rearrange("(p h) e d -> (h e) p d", h=2)).then_inc(const_loaded, DMA)

            def store_xt(b):
                sp.wait_ge(xt_ready, 2 * b + 2)
                sp.dma_start(xt_dram[:, b * S:(b + 1) * S], XST[b]).then_inc(xt_stored[b], DMA)
            store_xt(0)
            sp.wait_ge(xt_stored[0], DMA)
            sp.wait_ge(pool_const, 3)
            stage(sp, 1, 1)
            for c in range(2):
                sp.wait_ge(split_done, 2 * c + 2)
                for dst, src in spread_pairs(0):
                    part = slice(c * CH, (c + 1) * CH)
                    sp.dma_start(dst[:, :, part].bitcast(F32), src[:, :, part].bitcast(F32)).then_inc(qks_first[c], DMA)
            for b in range(1, B):
                store_xt(b)
            for b in range(1, B):
                sp.wait_ge(xt_stored[b], DMA)

            def body(it, half, par, first, last):
                if not last:
                    sp.wait_ge(v_filled, (it + 1) * 2)
                    stage(sp, it + 2, par)
                    spread(sp, it + 1, 1 - par)
            each_step(sp, body)
            sp.wait_ge(v_filled, STEPS * 2)
            sp.wait_ge(v_evac, STEPS * 2)
            sp.wait_ge(staged[0], staged_count(0, STEPS // 2))
            sp.wait_ge(zeroed, 1)
            col = lambda x: x.rearrange("(o p) -> p o", o=1)
            n = 0
            for dst, src in [(WE1_RAW[r], a["We1"].rearrange("e m h -> m e h")) for r in (slice(0, M), slice(M, P))] + \
                    [(W2, a["We2"].rearrange("e h m -> h e m")), (DECW, a["dec_W"].rearrange("(m p) d -> p m d", p=P)),
                     (C2SW[0:M], a["c2s_W"]), (C2SW[M:P], a["c2s_W"]), (ENCW, a["enc_W"]),
                     (S2CW[:, :, 0:M], a["s2c_W"].rearrange("(m p) c -> p m c", p=P)),
                     (S2CW[:, :, M:P], a["s2c_W"].rearrange("(m p) c -> p m c", p=P)),
                     (DECB, a["dec_b"].partition_broadcast(P)), (LNG, a["ln_g"].partition_broadcast(P)),
                     (LNBB, a["ln_b2"].partition_broadcast(P)),
                     (RW1_RAW[0:M, 0:M], a["rW1"]), (RW1_RAW[M:P, 0:M], a["rW1"]),
                     (RW1_RAW[0:M, M:P], a["rW1"]), (RW1_RAW[M:P, M:P], a["rW1"]),
                     (S2CB[0:M], col(a["s2c_b"])), (S2CB[M:P], col(a["s2c_b"])),
                     (RB1[0:M], col(a["rb1"])), (RB1[M:P], col(a["rb1"])),
                     (RW2[0:M], a["rW2"]), (RB2, a["rb2"].partition_broadcast(P)),
                     (ENCB, a["enc_b"].rearrange("(m p) -> p m", p=P)), (C2SB, a["c2s_b"].rearrange("(m p) -> p m", p=P)),
                     (BE1, a["be1"].rearrange("e h -> h e")), (BE2[0:E], a["be2"]),
                     (BE2[LOW:LOW + E], a["be2"])]:
                sp.dma_start(dst, src, allow_slow_non_contiguous=True).then_inc(f_loaded, DMA)
                n += 1
            assert n == FFN_LOADS
            out_tiles = out.rearrange("b (t p) d -> p (b t) d", p=P)

            def store(c):
                sp.wait_ge(f_out, c + 1)
                sp.dma_start(out_tiles[:, bass.ds(c * TC, TC), :], OUT).then_inc(stored, DMA)
            with sp.Fori(0, NC) as c:
                store(c)
            sp.wait_ge(stored, NC * DMA)

        def expand(gp, it, g):
            gp.wait_ge(rcp_done, it * 2 + g + 1)
            wait(gp, r_filled, it * 2 + (1 if g else -1))
            gp.nop(nofuse=True)
            gp.tensor_copy(RX[g][:, :, :, :], RCP[:, g, :].rearrange("p (t h) -> p t h", h=2).unsqueeze(3).broadcast_to([P, TC, 2, DH])).then_inc(rx_ready, 1)

        def split(gp, it, half_prev, par_prev, parts):
            if isinstance(it, int) and it == 1 and 0 in parts:
                gp.wait_ge(qks_first[0], SPREADS * DMA)
                gp.wait_ge(qks_first[1], SPREADS * DMA)
            elif half_prev is not None and 0 in parts:
                gp.wait_ge(qks_ready[par_prev], spread_count(par_prev, half_prev))
            for s in parts:
                h, c = s % 2, s // 2
                part = slice(c * CH, (c + 1) * CH)
                gp.wait_ge(qk_evac, it * 4 + s + 1)
                if half_prev is not None:
                    gp.nop(nofuse=True)
                    gp.tensor_copy(RH[:, h, part], RAW[:, s % 2, :]).then_inc(rounded, 1)
                gp.wait_ge(rounded, it * 4 + s + 1)
                gp.tensor_tensor(RL[:, h, part], RAW[:, s % 2, :], RH[:, h, part].bitcast(F32), ALU.subtract).then_inc(split_done, 1)

        @block.gpsimd
        def _(gp):
            gp.memset(IDENT[:, :], 0.0).then_inc(mask_step, 1)
            gp.memset(MASK[:, :], 0.0).then_inc(mask_step, 1)
            gp.wait_ge(mask_step, 2)
            gp.affine_select(out=IDENT[:, :], in_=IDENT[:, :], compare_op=ALU.not_equal, fill=1.0,
                             base=0, pattern=[[-1, P]], channel_multiplier=1).then_inc(pool_const, 1)
            gp.affine_select(out=MASK[:, S - P:S], in_=MASK[:, S - P:S], compare_op=ALU.is_ge, fill=BIG,
                             base=0, pattern=[[-1, P]], channel_multiplier=1).then_inc(pool_const, 1)
            gp.memset(LOWER[:, :, :], 1.0).then_inc(lower_set, 1)
            gp.wait_ge(lower_set, 1)
            gp.affine_select(out=LOWER[:, :, :], in_=LOWER[:, :, :], compare_op=ALU.is_gt, fill=0.0,
                             base=0, pattern=[[1, E], [-1, E]], channel_multiplier=0).then_inc(lower_set, 1)
            gp.wait_ge(bqk_loaded, 2 * DMA)
            gp.wait_ge(scale_set, 4)
            gp.tensor_scalar(BQK[:, :], BQK[:, :], QKSCALE[:, 0:1], None, ALU.mult).then_inc(pool_const, 1)
            split(gp, 0, None, None, range(4))
            gp.wait_ge(const_loaded, 4 * DMA)
            for b in range(B):
                gp.wait_ge(ln_y, 2 * b + 2)
                gp.tensor_tensor(X[:, b * QT:(b + 1) * QT, :], X[:, b * QT:(b + 1) * QT, :],
                                 BO[:, :].unsqueeze(1).broadcast_to([P, QT, D]), ALU.add).then_inc(bo_added, 1)

            def body(it, half, par, first, last):
                if not last:
                    split(gp, it + 1, half, par, (0, 1))
                if not first:
                    expand(gp, it - 1, 1)
                if not last:
                    split(gp, it + 1, half, par, (2, 3))
                expand(gp, it, 0)
            each_step(gp, body)

            def norm_in(c, k):
                wait(gp, f_turned, k)
                gp.tensor_tensor(YF, X[:, bass.ds(c * TC, TC), :],
                                 FMV[:, bass.ds(c * TC, TC), 0:1].broadcast_to([P, TC, D]), ALU.subtract).then_inc(f_centred, 1)
                gp.wait_ge(f_centred, k + 1)
                gp.tensor_tensor(YF, YF, FRS[:, bass.ds(c * TC, TC)].unsqueeze(2).broadcast_to([P, TC, D]), ALU.mult).then_inc(f_y, 1)

            def finish(c):
                gp.wait_ge(g_y, c + 1)
                gp.tensor_tensor(PRO, NRM, LNG.unsqueeze(1).broadcast_to([P, TC, D]), ALU.mult).then_inc(nrm_free, 1)
                gp.wait_ge(nrm_free, c + 2)
                gp.tensor_tensor(OUT, PRO, LNBB.unsqueeze(1).broadcast_to([P, TC, D]), ALU.add).then_inc(f_shifted, 1)
                gp.wait_ge(f_shifted, c + 1)
                gp.tensor_tensor(OUT, OUT, X[:, bass.ds(c * TC, TC), :], ALU.add).then_inc(f_out, 1)
                gp.wait_ge(stored, (c + 1) * DMA)
            gp.wait_ge(f_weights, 1)
            gp.tensor_tensor(SPREAD[0:2 * LOW], IDENT[0:2 * LOW, 0:E].unsqueeze(2).broadcast_to([2 * LOW, E, P]),
                             IDENT[0:2 * LOW, LOW:LOW + E].unsqueeze(2).broadcast_to([2 * LOW, E, P]), ALU.add).then_inc(f_spread, 1)
            gp.wait_ge(f_rs, 1)
            norm_in(0, 0)
            expand(gp, STEPS - 1, 1)
            norm_in(1, 1)
            gp.wait_ge(exp_done, STEPS * UNITS)
            gp.memset(PRO[:, 0, 0:1], 0.0).then_inc(nrm_free, 1)

            def chunk(c, par, first, last):
                if not last:
                    norm_in((c + 2) % NC, c + 2)
                if first:
                    gp.wait_ge(f_rs, 2)
                else:
                    finish(c - 1)
            each_chunk(gp, chunk)
            finish(NC - 1)

        def turn_norm(pe, b):
            for r in range(2):
                pe.wait_ge(ln_y, 2 * b + r + 1)
                if b == 2:
                    pe.wait_ge(xt_ready, r + 1)
                for k in range(TC):
                    last = pe.transpose(NB[b][r][:, k * P:(k + 1) * P], NY[b][:, r * TC + k, :], IDENT[:, :])
                last.then_inc(xt_turned, 1)

        def pe_qk(pe, par, s, bank=MB):
            h, c = s % 2, s // 2
            pe.matmul(bank[:, :], WQK[par][:, h, :], XTB[par][:, c * CH:(c + 1) * CH], start=True, stop=True).then_inc(qk_filled, 1)

        def pe_v(pe, it, par, s, bank=MB):
            for k in range(TC):
                t = s * TC + k
                last = pe.matmul(bank[:, k * P:(k + 1) * P], XTB[par][:, t * P:(t + 1) * P],
                                 WV[:, bass.ds((it % HP) * 2, 2), :].rearrange("p h e -> p (h e)"), start=True, stop=True)
            last.then_inc(v_filled, 1)

        def pe_scores(pe, it, par, n):
            t, h = n // 2, n % 2
            w = (t + 1) * P
            for c0 in range(0, w, CH):
                wc = max(min(CH, w - c0), 256)
                pe.matmul(SP_[n % 2][:, c0:c0 + wc], QS[par][:, h, t * P:(t + 1) * P], KH[par][:, h, c0:c0 + wc], start=True, stop=False)
                last = pe.matmul(SP_[n % 2][:, c0:c0 + wc], QS[par][:, h, t * P:(t + 1) * P], KL[par][:, h, c0:c0 + wc], start=False, stop=True)
            last.then_inc(s_filled, 1)

        def pe_turn(pe, it, n):
            pe.wait_ge(exp_done, it * UNITS + n + 1)
            for idx, j0, nb in turns_of(n):
                wait(pe, t_copied_act if idx % 2 == 0 else t_copied_dve, it * HALF_TURNS + idx // 2)
                for k in range(nb):
                    last = pe.transpose(TB[idx % 2][:, k * P:(k + 1) * P], PR[n % 4][:, (j0 + k) * P:(j0 + k + 1) * P], IDENT[:, :])
                last.then_inc(t_filled, 1)

        def pe_values(pe, it, par, g, j):
            if j == 0:
                done = it * HALF_TURNS + (4 if g == 0 else HALF_TURNS)
                pe.wait_ge(t_copied_act, done)
                pe.wait_ge(t_copied_dve, done)
                pe.wait_ge(v_evac, (it + 1) * 2)
                wait(pe, zn_done, it * 2 + g)
            off = (j - g * TC) * P if j >= g * TC else 0
            nj = (g + 1) * TC
            for h in range(2):
                last = pe.matmul(Z[h * DH:(h + 1) * DH, off:CH], V[par][:, j, h * DH:(h + 1) * DH], PT[g][:, h, j, off:CH],
                                 start=(j == 0), stop=(j == nj - 1))
            if j == nj - 1:
                last.then_inc(pv_done, 1)

        def pe_spread_sums(pe, it, g):
            pe.wait_ge(rx_ready, it * 2 + g + 1)
            for i in range(TC):
                last = pe.transpose(MB[:, i * P:(i + 1) * P], RX[g][:, i, :, :].rearrange("p h e -> p (h e)"), IDENT[:, :])
            last.then_inc(r_filled, 1)

        def pe_out(pe, it, g):
            pe.wait_ge(zn_done, it * 2 + g + 1)
            for i in range(TC):
                last = pe.matmul(MB[:, i * P:(i + 1) * P], ZN[g][:, i * P:(i + 1) * P],
                                 WO[:, bass.ds(it % HP, 1), :].rearrange("p o d -> p (o d)"), start=True, stop=True)
            last.then_inc(out_filled, 1)

        def pe_slot(pe, it, half, par, first, last, n):
            if n == 0:
                pe.wait_ge(qks_first[0], SPREADS * DMA) if first else pe.wait_ge(qks_ready[par], spread_count(par, half))
            if n == 8 and first:
                pe.wait_ge(qks_first[1], SPREADS * DMA)
            wait(pe, s_masked, it * UNITS + n - 1)
            pe_scores(pe, it, par, n)
            if n < 4 and not last:
                if n == 0:
                    pe.wait_ge(v_evac, it * 2 + 2)
                    nhalf = half + 1 if par else half
                    pe.wait_ge(staged[1 - par], staged_count(1 - par, nhalf))
                else:
                    pe.wait_ge(qk_evac, it * 4 + 4 + n)
                pe_qk(pe, 1 - par, n)
            if n == 5 and not first:
                if last:
                    pe.wait_ge(v_evac, it * 2 + 2)
                else:
                    pe.wait_ge(qk_evac, it * 4 + 8)
                pe_out(pe, it - 1, 0)
            if n == 7 and not first:
                pe.wait_ge(out_evac, it * 2 - 1)
                pe_spread_sums(pe, it - 1, 1)
            if n == 12:
                if first:
                    pe.wait_ge(qk_evac, 8)
                else:
                    pe.wait_ge(r_evac, it * 2)
                pe_spread_sums(pe, it, 0)
            if n == 13 and not first:
                pe.wait_ge(r_evac, it * 2 + 1)
                pe_out(pe, it - 1, 1)
            if n in (14, 15) and not last:
                if n == 14 and first:
                    pe.wait_ge(r_evac, 1)
                elif n == 14:
                    pe.wait_ge(out_evac, it * 2)
                else:
                    pe.wait_ge(v_evac, it * 2 + 3)
                pe_v(pe, it + 1, 1 - par, n - 14)
            if first and n == 0:
                turn_norm(pe, B - 1)
            if n == 3 and first:
                pe.wait_ge(xt_ready, 2 * B)
            if n >= 3:
                pe_turn(pe, it, n - 3)
            elif not first:
                pe_turn(pe, it - 1, UNITS + n - 3)
            if n in VALUES_BEFORE and not first:
                g, blocks = VALUES_BEFORE[n]
                for j in blocks:
                    pe_values(pe, it - 1, 1 - par, g, j)
            for j in VALUES.get(n, ()):
                pe_values(pe, it, par, 0, j)

        def pe_norm_turn(pe, k):
            pe.wait_ge(f_y, k + 1)
            wait(pe, f_t1, k)
            for i in range(TC):
                last = pe.transpose(A0[:, i * P:(i + 1) * P], YF[:, i, :], IDENT[:, :])
            last.then_inc(f_turned, 1)

        def pe_encode(pe, c):
            pe.wait_ge(f_yt, c + 1)
            wait(pe, gate_step, c * GSTEPS - GSTEPS + 1)
            for m, bank in ((0, A1), (1, A0)):
                pe.matmul(bank, ENCW[:, m * P:(m + 1) * P], YT, start=True, stop=True).then_inc(f_enc, 1)

        def pe_cont(pe, c):
            pe.wait_ge(f_et, c * 2 + 2)
            for m in range(HB):
                last = pe.matmul(A1, S2CW[:, m, :], ET[m], start=(m == 0), stop=(m == HB - 1))
            last.then_inc(f_s2c, 1)

        def pe_router(pe, c, par):
            pe.wait_ge(f_cl, c + 1)
            pe.matmul(A0, RW1, CH_[par], start=True, stop=False)
            pe.matmul(A0, RW1, CL_[par], start=False, stop=True).then_inc(f_r1, 1)

        def pe_logits(pe, c):
            pe.wait_ge(f_t1, c + 1)
            for k in range(TC):
                last = pe.matmul(A1[:, k * E:(k + 1) * E], T1[:, k * P:(k + 1) * P], RW2, start=True, stop=True)
            last.then_inc(f_lg, 1)

        def pe_gate_turn(pe, c):
            pe.wait_ge(f_gates, c + 1)
            wait(pe, f_gh, c * E - 1)
            for k in range(TC):
                last = pe.transpose(GB[0][:, k * P:(k + 1) * P], GP[:, k, :], IDENT[:, :])
            last.then_inc(f_gt, 1)

        def pe_hidden(pe, c, par, e):
            wait(pe, f_relu, c * E + e - 1)
            pe.matmul(TB[e % 2][:, :], WE1[:, e, :], CH_[par], start=True, stop=False)
            pe.matmul(TB[e % 2][:, :], WE1[:, e, :], CL_[par], start=False, stop=True).then_inc(f_h, 1)

        def pe_gates(pe, c, e):
            if e == 0:
                pe.wait_ge(f_glow, c + 1)
            wait(pe, f_gh, c * E + e - 1)
            pe.matmul(GB[e % 2], SPREAD[0:2 * LOW, e, :], GSTACK[0:2 * LOW], start=True, stop=True).then_inc(f_g, 1)

        def pe_experts(pe, c, p):
            pe.wait_ge(f_gh, c * E + 2 * p + 2)
            if p == 0:
                wait(pe, f_o, c)
            for e in (2 * p, 2 * p + 1):
                last = pe.matmul(Z[(e % 2) * M:(e % 2 + 1) * M, :], W2[:, e, :], GH[e % 4], start=(p == 0), stop=(e == E - 1))
            if p == E // 2 - 1:
                for be2 in (BE2H, BE2L):
                    last = pe.matmul(Z[0:M, :], be2[0:2 * LOW], GSTACK[0:2 * LOW], start=False, stop=be2 is BE2L)
            last.then_inc(f_w2, 1)

        def pe_c2s(pe, c, m, bank=MB):
            if m == 0:
                pe.wait_ge(f_o, c + 1)
            elif bank is MB:
                pe.wait_ge(f_smt, c * 2 + 1)
            pe.matmul(bank[:, :], C2SW[:, m * P:(m + 1) * P], O, start=True, stop=True).then_inc(f_c2s, 1)

        def pe_decode(pe, c):
            pe.wait_ge(f_smt, c * 2 + 2)
            for k in range(TC):
                for m in range(HB):
                    last = pe.matmul(MB[:, k * P:(k + 1) * P], SMT[m][:, k * P:(k + 1) * P], DECW[:, m, :], start=(m == 0), stop=(m == HB - 1))
            last.then_inc(f_dec, 1)

        @block.tensor
        def _(pe):
            pe.wait_ge(pool_const, 1)
            turn_norm(pe, 0)
            pe.wait_ge(staged[0], staged_count(0, 0))
            for s in range(4):
                pe.wait_ge(xt_ready, 1 + s // 2)
                if s >= 2:
                    pe.wait_ge(rounded, s - 1)
                pe_qk(pe, 0, s, (MB, Z)[s % 2])
            turn_norm(pe, 1)
            turn_norm(pe, 2)
            pe.wait_ge(const_loaded, 4 * DMA)
            pe.wait_ge(rounded, 4)
            pe_v(pe, 0, 0, 0)
            pe_v(pe, 0, 0, 1, Z)
            pe.wait_ge(xt_ready, 2 * B - 2)

            def body(it, half, par, first, last):
                for n in range(UNITS):
                    pe_slot(pe, it, half, par, first, last, n)
            each_step(pe, body)
            it, par = STEPS - 1, 1
            pe_turn(pe, it, UNITS - 3)
            pe_values(pe, it, par, 0, 2)
            pe_values(pe, it, par, 0, 3)
            pe.wait_ge(s_masked, STEPS * UNITS)
            pe.wait_ge(f_weights, 7)
            pe.matmul(GB[0][:, 0:D], ONES, DECW[:, 0, :], start=True, stop=False)
            pe.matmul(GB[0][:, 0:D], ONES, DECW[:, 1, :], start=False, stop=True)
            pe.matmul(GB[0][:, D:D + 8], S2CW[:, 0, :], ONES[:, 0:8], start=True, stop=False)
            pe.matmul(GB[0][:, D:D + 8], S2CW[:, 1, :], ONES[:, 0:8], start=False, stop=True).then_inc(f_sums, 1)
            pe_norm_turn(pe, 0)
            pe_turn(pe, it, UNITS - 2)
            pe_encode(pe, 0)
            pe_turn(pe, it, UNITS - 1)
            pe.wait_ge(r_evac, STEPS * 2 - 1)
            pe_out(pe, it, 0)
            for j in (0, 1):
                pe_values(pe, it, par, 1, j)
            pe_cont(pe, 0)
            for j in (2, 3, 4):
                pe_values(pe, it, par, 1, j)
            pe_router(pe, 0, 0)
            for j in (5, 6):
                pe_values(pe, it, par, 1, j)
            pe_logits(pe, 0)
            pe_values(pe, it, par, 1, 7)
            pe.wait_ge(out_evac, STEPS * 2 - 1)
            pe_spread_sums(pe, STEPS - 1, 1)
            pe_norm_turn(pe, 1)
            pe.wait_ge(r_evac, STEPS * 2)
            pe_out(pe, it, 1)

            pe.wait_ge(t_copied_act, STEPS * HALF_TURNS)
            pe.wait_ge(t_copied_dve, STEPS * HALF_TURNS)
            pe.wait_ge(f_biases, 2)

            def chunk(c, par, first, last):
                for e in (0, 1):
                    pe_hidden(pe, c, par, e)
                if not first:
                    pe_c2s(pe, c - 1, 0)
                pe_gate_turn(pe, c)
                if not last:
                    pe_encode(pe, c + 1)
                if first:
                    pe.wait_ge(f_spread, 1)
                else:
                    pe_c2s(pe, c - 1, 1)
                for e in (0, 1):
                    pe_gates(pe, c, e)
                for e in (2, 3):
                    pe_hidden(pe, c, par, e)
                if not last:
                    pe_cont(pe, c + 1)
                for e in (2, 3):
                    pe_gates(pe, c, e)
                pe_experts(pe, c, 0)
                if first:
                    pe.wait_ge(out_evac, STEPS * 2)
                else:
                    pe_decode(pe, c - 1)
                for e in (4, 5):
                    pe_hidden(pe, c, par, e)
                if not last:
                    pe_router(pe, c + 1, 1 - par)
                for e in (4, 5):
                    pe_gates(pe, c, e)
                pe_experts(pe, c, 1)
                if not last:
                    pe_logits(pe, c + 1)
                for e in (6, 7):
                    pe_hidden(pe, c, par, e)
                for e in (6, 7):
                    pe_gates(pe, c, e)
                pe_experts(pe, c, 2)
                if not last:
                    pe_norm_turn(pe, c + 2)
                pe_experts(pe, c, 3)
            each_chunk(pe, chunk)
            pe_c2s(pe, NC - 1, 0)
            pe_c2s(pe, NC - 1, 1, A0)
            pe_decode(pe, NC - 1)

        def copy_turn(eng, which, it, n):
            t, h = n // 2, n % 2
            g, tq = t // TC, t % TC
            if isinstance(it, int) and it == 0 and n == UNITS // 2:
                for b in range(1, B):
                    eng.wait_ge(xt_stored[b], DMA)
            for idx, j0, nb in turns_of(n):
                if idx % 2 == which:
                    eng.wait_ge(t_filled, it * TURNS + idx + 1)
                    dst = PT[g][:, h, j0:j0 + nb, tq * P:(tq + 1) * P]
                    src = TB[idx % 2][:, 0:nb * P].rearrange("p (j q) -> p j q", q=P)
                    if which == 0:
                        eng.activation(dst, src, ACT.Copy).then_inc(t_copied_act, 1)
                    else:
                        eng.tensor_copy(dst, src).then_inc(t_copied_dve, 1)

        def dve_reciprocal(v, it, g, par):
            v.wait_ge(exp_done, it * UNITS + 8 * g + 8)
            wait(v, rx_ready, it * 2 + (1 if g else -1))
            c0 = par * UNITS + g * 8
            v.reciprocal(RCP[:, g, :], L[:, c0:c0 + 8]).then_inc(rcp_done, 1)

        def dve_zn(v, it, g):
            v.wait_ge(pv_done, it * 2 + g + 1)
            v.wait_ge(r_evac, it * 2 + g + 1)
            v.tensor_tensor(ZN[g][:, :], Z[:, :], RSB[g][:, :], ALU.mult).then_inc(zn_done, 1)

        def dve_out(v, it, g):
            v.wait_ge(out_filled, it * 2 + g + 1)
            xs = X[:, bass.ds((it // HP) * QT + g * TC, TC), :]
            v.tensor_tensor(xs, xs, MB[:, :].rearrange("p (t d) -> p t d", d=D), ALU.add).then_inc(out_evac, 1)

        def dve_v(v, it, par, s, bank=MB):
            v.wait_ge(v_filled, it * 2 + s + 1)
            wait(v, pv_done, (it - 1) * 2)
            v.tensor_tensor(V[par][:, s * TC:(s + 1) * TC, :], bank[:, :].rearrange("p (t d) -> p t d", d=P),
                            BV[:, bass.ds((it % HP) * P, P)].unsqueeze(1).broadcast_to([P, TC, P]), ALU.add).then_inc(v_evac, 1)

        def dve_prepare(v, n):
            if n == 0:
                v.wait_ge(f_high, 2)
                v.tensor_tensor(QS[0][M:P, 0, :], XTB[0][M:P, :], HIGH[M:P].bitcast(F32), ALU.subtract).then_inc(f_weights, 1)
            if n == 1:
                v.wait_ge(f_high, 4)
                v.tensor_tensor(RW1[M:P], RW1_RAW[M:P], HIGH1[M:P].bitcast(F32), ALU.subtract).then_inc(f_weights, 1)
                v.tensor_copy(BE2H[0:2 * LOW], BE2[0:2 * LOW]).then_inc(f_high, 1)
                v.wait_ge(f_high, 5)
                v.tensor_tensor(BE2L[0:2 * LOW], BE2[0:2 * LOW], BE2H[0:2 * LOW].bitcast(F32), ALU.subtract).then_inc(f_weights, 1)
                for w in (ENCB, C2SB, S2CW, DECW):
                    v.tensor_scalar(w, w, 0.5, None, ALU.mult).then_inc(f_weights, 1)

        def dve_biases(v):
            v.wait_ge(f_sums, 1)
            v.tensor_tensor(DECB, DECB, GB[0][:, 0:D], ALU.add).then_inc(f_biases, 1)
            v.tensor_tensor(S2CB, S2CB, GB[0][:, D:D + 1], ALU.add).then_inc(f_biases, 1)

        def f_norm_stats(v, tiles):
            for t in tiles:
                v.bn_stats(FST[:, t, :], X[:, t, :]).then_inc(f_stats, 1)
            for t in tiles:
                v.wait_ge(f_stats, t + 1)
                v.bn_aggr(FMV[:, t, :], FST[:, t, :]).then_inc(f_aggr, 1)

        def f_norm_scale(v, i):
            v.wait_ge(f_sd, i + 1)
            v.reciprocal(FRS[:, FNORM[i]], FSD[:, FNORM[i]]).then_inc(f_rs, 1)

        def dve_slot(v, it, half, par, first, last, n):
            w = (n // 2 + 1) * P
            v.wait_ge(s_filled, it * UNITS + n + 1)
            wait(v, exp_done, it * UNITS + n - 1)
            v.nop(nofuse=True)
            v.tensor_tensor_reduce(out=SSB[n % 2][:, 0:w], in0=SP_[n % 2][:, 0:w], in1=MASK[:, S - w:S], scale=1.0, scalar=BIG,
                                   op0=ALU.add, op1=ALU.min, accum_out=NM[:, par * UNITS + n:par * UNITS + n + 1]).then_inc(s_masked, 1)
            if not first:
                if n == 1:
                    dve_zn(v, it - 1, 0)
                    dve_reciprocal(v, it - 1, 1, 1 - par)
                if n == 5:
                    v.wait_ge(bo_added, B)
                    dve_out(v, it - 1, 0)
                if n == 11:
                    dve_zn(v, it - 1, 1)
                if n == 13:
                    dve_out(v, it - 1, 1)
            if n == 9:
                dve_reciprocal(v, it, 0, par)
            if n in (14, 15) and not last:
                dve_v(v, it + 1, 1 - par, n - 14)
            if last and n == 0:
                v.wait_ge(v_evac, STEPS * 2)
                v.memset(BV[:, 0:P], 0.0).then_inc(zeroed, 1)
                v.memset(ONES, 1.0).then_inc(zeroed, 1)
                v.wait_ge(qks_ready[1], spread_count(1, half))
                v.memset(GP, 0.0).then_inc(zeroed, 1)
            if last and n in (12, 14):
                dve_prepare(v, (n - 12) // 2)
            if last and n == 15:
                f_norm_scale(v, 0)
            if n >= 3:
                copy_turn(v, 1, it, n - 3)
            elif not first:
                copy_turn(v, 1, it - 1, UNITS + n - 3)
            if last and 1 <= n <= 8:
                if n == 1:
                    v.wait_ge(out_evac, (STEPS - QT) * 2)
                f_norm_stats(v, range(3 * n - 3, 3 * n))

        def gates_1(v, c):
            v.wait_ge(f_lg, c + 1)
            s = c * GSTEPS
            v.tensor_tensor(LG, per(A1[:, 0:TC * E]), RB2.unsqueeze(1).broadcast_to([P, TC, E]), ALU.add).then_inc(gate_step, 1)
            v.wait_ge(gate_step, s + 1)
            v.tensor_reduce(MX, LG, AXIS_X, ALU.max).then_inc(gate_step, 1)
            v.wait_ge(gate_step, s + 2)
            v.tensor_tensor(LM, LG, MX.unsqueeze(2).broadcast_to([P, TC, E]), ALU.subtract).then_inc(gate_step, 1)

        def gates_2(v, c, beside):
            s = c * GSTEPS + 3
            over = lambda x: x.unsqueeze(2).broadcast_to([P, TC, E])
            first = PB.unsqueeze(3).broadcast_to([P, TC, E, E])
            other = PB.unsqueeze(2).broadcast_to([P, TC, E, E])

            def step(op, n):
                op.then_inc(gate_step, 1)
                if n in beside:
                    beside[n]()
                v.wait_ge(gate_step, s + n)
            v.wait_ge(f_ex, c + 1)
            step(v.tensor_reduce(SUM, EX, AXIS_X, ALU.add), 1)
            step(v.reciprocal(RSUM, SUM), 2)
            step(v.tensor_tensor(PB, EX, over(RSUM), ALU.mult), 3)
            step(v.tensor_tensor(EQ, other, first, ALU.is_equal), 4)
            step(v.tensor_tensor(EQ, EQ, LOWER[:, :, :].unsqueeze(1).broadcast_to([P, TC, E, E]), ALU.mult), 5)
            step(v.tensor_tensor(GR, other, first, ALU.is_gt), 6)
            step(v.tensor_tensor(GR, GR, EQ, ALU.add), 7)
            step(v.tensor_reduce(RK, GR, AXIS_X, ALU.add), 8)
            step(v.scalar_tensor_tensor(G1, RK, 1.5, PB, ALU.is_lt, ALU.mult), 9)
            step(v.tensor_reduce(GS, G1, AXIS_X, ALU.add), 10)
            step(v.reciprocal(RG, GS), 11)
            wait(v, f_gt, c)
            v.tensor_tensor(twice(GP), G1.unsqueeze(2).broadcast_to([P, TC, 2, E]),
                            RG.unsqueeze(2).unsqueeze(3).broadcast_to([P, TC, 2, E]), ALU.mult).then_inc(f_gates, 1)

        def dve_gates_low(v, c):
            low = slice(LOW, 2 * LOW)
            v.wait_ge(f_ghigh, c + 1)
            v.tensor_tensor(GSTACK[low], GB[0][low], GSTACK[low].bitcast(F32), ALU.subtract).then_inc(f_glow, 1)

        def dve_low(v, c, par):
            v.wait_ge(f_c32, c * 2 + 2)
            v.tensor_tensor(CL_[par], C32, CH_[par].bitcast(F32), ALU.subtract).then_inc(f_cl, 1)

        def dve_gate(v, c, e):
            v.wait_ge(f_relu, c * E + e + 1)
            v.wait_ge(f_g, c * E + e + 1)
            wait(v, f_w2, c * 4 + e // 2 - 1)
            v.tensor_tensor(GH[e % 4], H[e % 2], GB[e % 2], ALU.mult).then_inc(f_gh, 1)

        def dve_decoded(v, c):
            v.wait_ge(f_dec, c + 1)
            v.tensor_tensor(DD, tiled(MB[:, :]), DECB.unsqueeze(1).broadcast_to([P, TC, D]), ALU.add).then_inc(f_d, 1)

        def dve_out_stats(v, c):
            v.wait_ge(f_dt, c + 1)
            for k in range(TC):
                v.bn_stats(ST2[:, k, :], DT[:, k, :]).then_inc(g_stats, 1)
            for k in range(TC):
                v.wait_ge(g_stats, c * TC + k + 1)
                v.nop(nofuse=True)
                v.bn_aggr(MV2[:, k, :], ST2[:, k, :]).then_inc(g_aggr, 1)

        def dve_out_norm(v, c):
            v.wait_ge(g_sd, c + 1)
            v.reciprocal(RS2[:, :], SD2[:, :]).then_inc(g_rs, 1)
            v.wait_ge(g_rs, c + 1)
            v.wait_ge(nrm_free, c + 1)
            for k in range(TC):
                last = v.tensor_scalar(NRM[:, k, :], DT[:, k, :], MV2[:, k, 0:1], RS2[:, k:k + 1], ALU.subtract, ALU.mult)
            last.then_inc(g_y, 1)

        @block.vector
        def _(v):
            v.memset(QKSCALE[0:DH, :], -(DH ** -0.5)).then_inc(scale_set, 1)
            v.memset(QKSCALE[DH:P, :], 1.0).then_inc(scale_set, 1)
            v.memset(EPST[:, :], EPS).then_inc(scale_set, 1)
            v.memset(EPS4[:, :], 4 * EPS).then_inc(scale_set, 1)

            def norm_stats(b):
                v.wait_ge(x_loaded[b], DMA)
                for k in range(b * QT, (b + 1) * QT):
                    v.bn_stats(NST[:, k, :], X[:, k, :]).then_inc(ln_stats, 1)
                for k in range(b * QT, (b + 1) * QT):
                    v.wait_ge(ln_stats, k + 1)
                    v.bn_aggr(NMV[:, k, :], NST[:, k, :]).then_inc(ln_aggr, 1)

            def norm_scale(i, t):
                def step(op, n):
                    op.then_inc(ln_step, 1)
                    v.wait_ge(ln_step, i * 5 + n)
                v.wait_ge(ln_sd, 2 * i + 2)
                step(v.reciprocal(NRS[:, t], NSD[:, t]), 1)
                step(v.tensor_tensor(NVAR[:, t], NMV[:, t, 1], NRS[:, t], ALU.mult), 2)
                v.tensor_tensor(NVAR[:, t], NVAR[:, t], NRS[:, t], ALU.mult).then_inc(ln_step, 1)
                v.wait_ge(ln_sd, 2 * i + 3)
                step(v.reciprocal(NRS2[:, t], NSD2[:, t]), 4)
                step(v.tensor_tensor(NSCALE[:, t], NRS[:, t], NRS2[:, t], ALU.mult), 5)

            def norm_apply(b):
                if b == 2:
                    v.wait_ge(xt_turned, 2)
                for k in range(QT):
                    t = b * QT + k
                    op = v.tensor_scalar(NY[b][:, k, :], X[:, t, :], NMV[:, t, 0:1], NSCALE[:, t:t + 1], ALU.subtract, ALU.mult)
                    if k % TC == TC - 1:
                        op.then_inc(ln_y, 1)
            norm_stats(0)
            norm_scale(0, NORM_TILES[0])
            norm_apply(0)
            for b in range(1, B):
                norm_stats(b)
            norm_scale(1, NORM_TILES[1])
            v.wait_ge(const_loaded, 4 * DMA)
            norm_apply(1)
            norm_apply(2)
            dve_v(v, 0, 0, 0)
            dve_v(v, 0, 0, 1, Z)
            norm_apply(3)
            v.wait_ge(pool_const, 2)

            def body(it, half, par, first, last):
                for n in range(UNITS):
                    dve_slot(v, it, half, par, first, last, n)
            each_step(v, body)
            it = STEPS - 1
            dve_zn(v, it, 0)
            for n in range(3):
                copy_turn(v, 1, it, UNITS + n - 3)
            dve_reciprocal(v, it, 1, 1)
            dve_out(v, it, 0)
            dve_biases(v)
            v.wait_ge(out_evac, STEPS * 2 - 1)
            f_norm_stats(v, range(NT - QT, NT - TC))
            v.wait_ge(zeroed, 3)
            dve_low(v, 0, 0)
            gates_1(v, 0)
            gates_2(v, 0, {4: lambda: dve_zn(v, it, 1), 9: lambda: dve_out(v, it, 1)})

            def chunk(c, par, first, last):
                dve_gates_low(v, c)
                for e in range(4):
                    dve_gate(v, c, e)
                if not last:
                    dve_low(v, c + 1, 1 - par)
                if not first:
                    dve_decoded(v, c - 1)
                dve_gate(v, c, 4)
                dve_gate(v, c, 5)
                if first:
                    v.wait_ge(out_evac, STEPS * 2)
                    f_norm_stats(v, range(NT - TC, NT))
                else:
                    dve_out_stats(v, c - 1)
                if not last:
                    gates_1(v, c + 1)
                    gates_2(v, c + 1, {1: lambda: dve_gate(v, c, 6), 2: lambda: dve_gate(v, c, 7)})
                else:
                    dve_gate(v, c, 6)
                    dve_gate(v, c, 7)
                if first:
                    f_norm_scale(v, 1)
                else:
                    dve_out_norm(v, c - 1)
            each_chunk(v, chunk)
            dve_decoded(v, NC - 1)
            dve_out_stats(v, NC - 1)
            dve_out_norm(v, NC - 1)

        def norm_out(act, b):
            for r in range(2):
                act.wait_ge(xt_turned, 2 * b + r + 1)
                act.activation(XST[b][:, r * CH:(r + 1) * CH], NB[b][r], ACT.Identity,
                               bias=LNB[:, 0:1], scale=LNW[:, 0:1]).then_inc(xt_ready, 1)

        def act_qk(act, it, s, bias, bank=MB):
            h, c = s % 2, s // 2
            act.wait_ge(qk_filled, it * 4 + s + 1)
            wait(act, split_done, it * 4 + s - 1)
            act.activation(RAW[:, s % 2, :], bank[:, :], ACT.Identity, bias=bias[:, h:h + 1], scale=QKSCALE[:, 0:1]).then_inc(qk_evac, 1)

        def act_sums(act, it, g):
            act.wait_ge(r_filled, it * 2 + g + 1)
            wait(act, zn_done, it * 2 + (1 if g else -1))
            act.activation(RSB[g][:, :], MB[:, :], ACT.Copy).then_inc(r_evac, 1)

        def weight_halves(act, r):
            act.wait_ge(f_loaded, FFN_LOADS * DMA)
            raw, high, stack = ((XTB[0][:, :], HIGH, QS[0][:, 0, :]), (RW1_RAW, HIGH1, RW1))[r // 2]
            if r % 2 == 0:
                act.activation(high, raw, ACT.Copy).then_inc(f_high, 1)
            else:
                act.activation(stack[0:M], raw[0:M], ACT.Copy).then_inc(f_high, 1)

        def f_deviations(act, i):
            act.wait_ge(f_aggr, FNORM[i].stop)
            act.activation(FSD[:, FNORM[i]], FMV[:, FNORM[i], 1], ACT.Sqrt, bias=EPST[:, 0:1]).then_inc(f_sd, 1)

        def act_slot(act, it, half, par, first, last, n):
            if n < 4 and not last:
                act_qk(act, it + 1, n, BQKS[1 - par])
            if first and n == 0:
                norm_out(act, B - 1)
            if n == 7 and not first:
                act_sums(act, it - 1, 1)
            if n == 12:
                act_sums(act, it, 0)
            if last and 9 <= n <= 11:
                weight_halves(act, n - 9)
            if last and n == 12:
                weight_halves(act, 3)
            if last and n == 14:
                f_deviations(act, 0)
            if n >= 3:
                copy_turn(act, 0, it, n - 3)
            elif not first:
                copy_turn(act, 0, it - 1, UNITS + n - 3)
            w = (n // 2 + 1) * P
            col = par * UNITS + n
            act.wait_ge(s_masked, it * UNITS + n + 1)
            if n >= 4:
                act.wait_ge(t_filled, it * TURNS + turns_of(n - 4)[-1][0] + 1)
            elif not first:
                act.wait_ge(t_filled, (it - 1) * TURNS + turns_of(UNITS + n - 4)[-1][0] + 1)
            act.activation(PR[n % 4][:, 0:w], SSB[n % 2][:, 0:w], ACT.Exp, bias=NM[:, col:col + 1], scale=-1.0,
                           accum_out=L[:, col:col + 1]).then_inc(exp_done, 1)

        @block.scalar
        def _(act):
            act.wait_ge(scale_set, 4)
            act.activation(NSD2[:, 0:1], EPST[:, 0:1], ACT.Sqrt).then_inc(ln_sd, 1)

            def norm_deviations(i, t):
                act.wait_ge(ln_aggr, t.stop)
                act.activation(NSD[:, t], NMV[:, t, 1], ACT.Sqrt, bias=EPST[:, 0:1]).then_inc(ln_sd, 1)
                act.wait_ge(ln_step, i * 5 + 3)
                act.activation(NSD2[:, t], NVAR[:, t], ACT.Sqrt, bias=EPST[:, 0:1]).then_inc(ln_sd, 1)

            norm_deviations(0, NORM_TILES[0])
            act.wait_ge(ln_loaded, 2 * DMA)
            norm_out(act, 0)
            act.wait_ge(pool_const, 3)
            for s in range(4):
                act_qk(act, 0, s, BQK, (MB, Z)[s % 2])
                act.activation(RH[:, s % 2, (s // 2) * CH:(s // 2 + 1) * CH], (MB, Z)[s % 2][:, :], ACT.Identity,
                               bias=BQK[:, s % 2:s % 2 + 1], scale=QKSCALE[:, 0:1]).then_inc(rounded, 1)
                if s == 1:
                    norm_deviations(1, NORM_TILES[1])
            norm_out(act, 1)
            norm_out(act, 2)

            def body(it, half, par, first, last):
                for n in range(UNITS):
                    act_slot(act, it, half, par, first, last, n)
            each_step(act, body)
            it = STEPS - 1
            copy_turn(act, 0, it, UNITS - 3)

            def turned(k):
                act.wait_ge(f_turned, k + 1)
                act.activation(YT, A0, ACT.Copy).then_inc(f_yt, 1)

            def encoded(c):
                for m, bank in ((0, A1), (1, A0)):
                    act.wait_ge(f_enc, c * 2 + m + 1)
                    act.activation(ET[m], bank, ACT.Tanh, bias=ENCB[:, m:m + 1], scale=0.5).then_inc(f_et, 1)

            def cont(c, par):
                act.wait_ge(f_s2c, c + 1)
                wait(act, f_cl, c)
                act.activation(C32, A1, ACT.Identity, bias=S2CB).then_inc(f_c32, 1)
                act.activation(CH_[par], A1, ACT.Identity, bias=S2CB).then_inc(f_c32, 1)

            def routed(c):
                act.wait_ge(f_r1, c + 1)
                act.activation(T1, A0, ACT.Tanh, bias=RB1).then_inc(f_t1, 1)

            def exps(c):
                act.wait_ge(gate_step, c * GSTEPS + 3)
                act.activation(EX, LM, ACT.Exp).then_inc(f_ex, 1)

            def gates_high(c):
                act.wait_ge(f_gt, c + 1)
                act.activation(GSTACK[0:2 * LOW], GB[0][0:2 * LOW], ACT.Copy).then_inc(f_ghigh, 1)

            def hidden(c, e):
                act.wait_ge(f_h, c * E + e + 1)
                wait(act, f_gh, c * E + e - 1)
                act.activation(H[e % 2], TB[e % 2][:, :], ACT.Relu, bias=BE1[:, e:e + 1]).then_inc(f_relu, 1)

            def experts(c):
                act.wait_ge(f_w2, c * 4 + 4)
                act.activation(O, Z[:, :], ACT.Copy).then_inc(f_o, 1)

            def out_hidden(c, m, bank=MB):
                act.wait_ge(f_c2s, c * 2 + m + 1)
                act.activation(SMT[m], bank[:, :], ACT.Tanh, bias=C2SB[:, m:m + 1], scale=0.5).then_inc(f_smt, 1)

            def decoded(c):
                act.wait_ge(f_d, c + 1)
                act.activation(DT, DD, ACT.Tanh, scale=0.5).then_inc(f_dt, 1)

            def out_deviation(c):
                act.wait_ge(g_aggr, (c + 1) * TC)
                act.activation(SD2[:, :], MV2[:, :, 1], ACT.Sqrt, bias=EPS4[:, 0:1]).then_inc(g_sd, 1)

            act.wait_ge(f_weights, 7)
            turned(0)
            copy_turn(act, 0, it, UNITS - 2)
            copy_turn(act, 0, it, UNITS - 1)
            encoded(0)
            act.wait_ge(f_biases, 2)
            cont(0, 0)
            routed(0)
            exps(0)
            act_sums(act, it, 1)
            turned(1)

            def chunk(c, par, first, last):
                hidden(c, 0)
                hidden(c, 1)
                if not first:
                    out_hidden(c - 1, 0)
                gates_high(c)
                if not last:
                    encoded(c + 1)
                if not first:
                    out_hidden(c - 1, 1)
                hidden(c, 2)
                hidden(c, 3)
                if not last:
                    cont(c + 1, 1 - par)
                hidden(c, 4)
                hidden(c, 5)
                if not first:
                    decoded(c - 1)
                if not last:
                    routed(c + 1)
                hidden(c, 6)
                if not last:
                    exps(c + 1)
                hidden(c, 7)
                if first:
                    f_deviations(act, 1)
                else:
                    out_deviation(c - 1)
                if not last:
                    turned(c + 2)
                experts(c)
            each_chunk(act, chunk)
            out_hidden(NC - 1, 0)
            out_hidden(NC - 1, 1, A0)
            decoded(NC - 1)
            out_deviation(NC - 1)


_NAMES = {
    "x": "L0_attn_resid_stream", "W_q": "L0_attn_W_q", "W_k": "L0_attn_W_k", "W_v": "L0_attn_W_v", "W_o": "L0_attn_W_o",
    "b_q": "L0_attn_b_q", "b_k": "L0_attn_b_k", "b_v": "L0_attn_b_v", "b_o": "L0_attn_b_o", "ln_w": "L0_attn_ln_w",
    "ln_b": "L0_attn_ln_b", "enc_W": "L0_ffn_enc_W", "enc_b": "L0_ffn_enc_b", "s2c_W": "L0_ffn_s2c_W", "s2c_b": "L0_ffn_s2c_b",
    "rW1": "L0_ffn_rW1", "rb1": "L0_ffn_rb1", "rW2": "L0_ffn_rW2", "rb2": "L0_ffn_rb2", "We1": "L0_ffn_We1", "be1": "L0_ffn_be1",
    "We2": "L0_ffn_We2", "be2": "L0_ffn_be2", "c2s_W": "L0_ffn_c2s_W", "c2s_b": "L0_ffn_c2s_b", "dec_W": "L0_ffn_dec_W",
    "dec_b": "L0_ffn_dec_b", "ln_g": "L0_ffn_ln_g", "ln_b2": "L0_ffn_ln_b",
}


def kernel(**inputs):
    import concourse.bacc as bacc
    from concourse.bass_utils import run_bass_kernel_spmd

    nc = bacc.Bacc("TRN2", target_bir_lowering=False, num_devices=1)
    arrays, args = {}, {}
    for short, name in _NAMES.items():
        arr = np.ascontiguousarray(inputs[name])
        arrays[f"in_{short}"] = arr
        args[short] = nc.dram_tensor(f"in_{short}", arr.shape, mybir.dt.from_np(arr.dtype), kind="ExternalInput").ap()
    out = nc.dram_tensor("out_x", (B, S, D), F32, kind="ExternalOutput").ap()
    build_program(nc, args, out)
    r = run_bass_kernel_spmd(nc, [arrays], core_ids=[0])
    return r.results[0]["out_x"]
```
